# Optimizing a Trainium2 kernel written in Bass

```python
import numpy as np
import jax
import jax.numpy as jnp

def _softmax(x, axis=-1):
    return jax.nn.softmax(x, axis=axis)

def _gelu(x):
    return jax.nn.gelu(x, approximate=True)

def _silu(x):
    return jax.nn.silu(x)

def _sigmoid(x):
    return jax.nn.sigmoid(x)

def _layernorm(x, axis=-1, eps=1e-05):
    m = jnp.mean(x, axis=axis, keepdims=True)
    v = jnp.var(x, axis=axis, keepdims=True)
    return (x - m) / jnp.sqrt(v + eps)

def _scatter_add(tgt, idx, src, axis=0):
    return tgt.at[idx].add(src)

def _segment_sum(src, seg, n):
    return jax.ops.segment_sum(src, seg, n)
kernel_name = 'mk_cond_resid_d4_seqx_r8_6dbbe5'

def setup_inputs(seed: int=0):
    np.random.seed(seed)
    _w = jnp.asarray

    def _rec_inputs():
        import jax
        import jax.numpy as jnp
        _rk = jax.random.key(seed)
        x = 8.748e-05 + 1 * jax.random.normal(jax.random.fold_in(_rk, 1), (32, 32, 256), jnp.float32)
        _lenS = 32 - jax.random.randint(jax.random.fold_in(_rk, 7), (32,), 0, max(1, 32 // 4) + 1, jnp.int32)
        _lenS2 = 32 - jax.random.randint(jax.random.fold_in(_rk, 8), (32,), 0, max(1, 32 // 4) + 1, jnp.int32)
        cond_2048 = -9.80646e-05 + 1.00041 * jax.random.normal(jax.random.fold_in(_rk, 11), (32, 256), jnp.float32)
        return (x, cond_2048)
    x, cond_2048 = _rec_inputs()

    def _L0_cond_setup():
        import jax, jax.numpy as jnp
        import numpy as np
        DT = 0.01
        EPSILON = 0.08
        ALPHA = 0.7
        BETA = 0.8
        CLAMP = 20.0
        B, T, N = (32, 128, 256)

        def _derivative(q, p, drive, coupling, bias):
            i_couple = jnp.tanh(q) @ coupling.T
            dq = q - q ** 3 / 3.0 - p + drive + i_couple + bias
            dp = EPSILON * (q + ALPHA - BETA * p)
            return (dq, dp)

        def _rk4_step(q, p, drive, coupling, bias):
            dq1, dp1 = _derivative(q, p, drive, coupling, bias)
            dq2, dp2 = _derivative(q + 0.5 * DT * dq1, p + 0.5 * DT * dp1, drive, coupling, bias)
            dq3, dp3 = _derivative(q + 0.5 * DT * dq2, p + 0.5 * DT * dp2, drive, coupling, bias)
            dq4, dp4 = _derivative(q + DT * dq3, p + DT * dp3, drive, coupling, bias)
            q_next = q + DT / 6.0 * (dq1 + 2 * dq2 + 2 * dq3 + dq4)
            p_next = p + DT / 6.0 * (dp1 + 2 * dp2 + 2 * dp3 + dp4)
            q_next = jnp.clip(q_next, -CLAMP, CLAMP)
            p_next = jnp.clip(p_next, -CLAMP, CLAMP)
            return (q_next, p_next)
        key = jax.random.key(seed)
        k1, k2, k3, k4 = jax.random.split(key, 4)
        return {'q0': jax.random.normal(k1, (B, N), dtype=jnp.float32), 'p0': jax.random.normal(k2, (B, N), dtype=jnp.float32), 'input_drive_seq': jax.random.normal(k3, (B, T, N), dtype=jnp.float32), 'coupling': jax.random.normal(k4, (N, N), dtype=jnp.float32) * 0.01, 'bias': jnp.zeros((N,), dtype=jnp.float32)}
    _L0_cond_all = _L0_cond_setup()
    _L0_cond_in = {k: v for k, v in _L0_cond_all.items() if k in ('coupling', 'bias')}
    del _L0_cond_all

    def _L1_cond_setup():
        import jax, jax.numpy as jnp
        import numpy as np
        B, T, D = (16, 128, 256)
        key = jax.random.key(seed)
        k0, k1, k2, k3 = jax.random.split(key, 4)
        scale = 1.0 / np.sqrt(D)
        return {'initial_state': jax.random.normal(k0, (B, D), jnp.float32), 'inputs': jax.random.normal(k1, (B, T, D), jnp.float32), 'W_ih': jax.random.normal(k2, (D, 3 * D), jnp.float32) * scale, 'W_hh': jax.random.normal(k3, (D, 3 * D), jnp.float32) * scale, 'b_ih': jnp.zeros((3 * D,), jnp.float32), 'b_hh': jnp.zeros((3 * D,), jnp.float32)}
    _L1_cond_all = _L1_cond_setup()
    _L1_cond_in = {k: v for k, v in _L1_cond_all.items() if k in ('W_ih', 'W_hh', 'b_ih', 'b_hh')}
    del _L1_cond_all

    def _L2_cond_setup():
        import jax, jax.numpy as jnp
        import numpy as np
        N, C, L_IN, L_OUT = (32, 32, 256, 256)
        key = jax.random.key(seed)
        k1, k2 = jax.random.split(key)
        inp = jax.random.normal(k1, (N, C, L_IN), dtype=jnp.float32)
        grid = jax.random.uniform(k2, (N, L_OUT), dtype=jnp.float32) * 2.0 - 1.0
        return {'input': inp, 'grid': grid, 'padding_mode': 1, 'align_corners': 1}
    _L2_cond_all = _L2_cond_setup()
    _L2_cond_in = {k: v for k, v in _L2_cond_all.items() if k in ()}
    del _L2_cond_all

    def _L3_cond_setup():
        import jax, jax.numpy as jnp
        import numpy as np
        NUM_BLOCKS = 8
        NUM_LAYERS = 4
        EPS = 1e-06
        key = jax.random.key(seed)
        ks = jax.random.split(key, 6)
        B, S, H = (4, 512, 256)
        inputs = jax.random.normal(ks[0], (B, S, H), dtype=jnp.float32)
        query_vectors = jax.random.normal(ks[1], (NUM_LAYERS, H), dtype=jnp.float32) * 0.01
        lim = float(np.sqrt(6.0 / (H + H)))
        Wk = jax.random.uniform(ks[2], (H, H), minval=-lim, maxval=lim, dtype=jnp.float32)
        Wo = jax.random.uniform(ks[3], (H, H), minval=-lim, maxval=lim, dtype=jnp.float32)
        rms_weight = jnp.ones((H,), dtype=jnp.float32)
        ln_gamma = jnp.ones((H,), dtype=jnp.float32)
        ln_beta = jnp.zeros((H,), dtype=jnp.float32)
        return {'inputs': inputs, 'layer_idx': 1, 'rms_weight': rms_weight, 'query_vectors': query_vectors, 'Wk': Wk, 'Wo': Wo, 'ln_gamma': ln_gamma, 'ln_beta': ln_beta}
    _L3_cond_all = _L3_cond_setup()
    _L3_cond_in = {k: v for k, v in _L3_cond_all.items() if k in ('rms_weight', 'Wk', 'Wo', 'ln_gamma', 'ln_beta')}
    del _L3_cond_all
    return {'x': x, 'cond_2048': cond_2048, 'L0_cond_coupling': _L0_cond_in['coupling'], 'L0_cond_bias': _L0_cond_in['bias'], 'L1_cond_W_ih': _L1_cond_in['W_ih'], 'L1_cond_W_hh': _L1_cond_in['W_hh'], 'L1_cond_b_ih': _L1_cond_in['b_ih'], 'L1_cond_b_hh': _L1_cond_in['b_hh'], 'L3_cond_rms_weight': _L3_cond_in['rms_weight'], 'L3_cond_Wk': _L3_cond_in['Wk'], 'L3_cond_Wo': _L3_cond_in['Wo'], 'L3_cond_ln_gamma': _L3_cond_in['ln_gamma'], 'L3_cond_ln_beta': _L3_cond_in['ln_beta']}

def reference(x, cond_2048, L0_cond_coupling, L0_cond_bias, L1_cond_W_ih, L1_cond_W_hh, L1_cond_b_ih, L1_cond_b_hh, L3_cond_rms_weight, L3_cond_Wk, L3_cond_Wo, L3_cond_ln_gamma, L3_cond_ln_beta):
    import jax
    import jax.numpy as jnp

    def _L0_cond_ref(q0, p0, input_drive_seq, coupling, bias):
        import jax, jax.numpy as jnp
        import numpy as np
        DT = 0.01
        EPSILON = 0.08
        ALPHA = 0.7
        BETA = 0.8
        CLAMP = 20.0
        B, T, N = (32, 128, 256)

        def _derivative(q, p, drive, coupling, bias):
            i_couple = jnp.tanh(q) @ coupling.T
            dq = q - q ** 3 / 3.0 - p + drive + i_couple + bias
            dp = EPSILON * (q + ALPHA - BETA * p)
            return (dq, dp)

        def _rk4_step(q, p, drive, coupling, bias):
            dq1, dp1 = _derivative(q, p, drive, coupling, bias)
            dq2, dp2 = _derivative(q + 0.5 * DT * dq1, p + 0.5 * DT * dp1, drive, coupling, bias)
            dq3, dp3 = _derivative(q + 0.5 * DT * dq2, p + 0.5 * DT * dp2, drive, coupling, bias)
            dq4, dp4 = _derivative(q + DT * dq3, p + DT * dp3, drive, coupling, bias)
            q_next = q + DT / 6.0 * (dq1 + 2 * dq2 + 2 * dq3 + dq4)
            p_next = p + DT / 6.0 * (dp1 + 2 * dp2 + 2 * dp3 + dp4)
            q_next = jnp.clip(q_next, -CLAMP, CLAMP)
            p_next = jnp.clip(p_next, -CLAMP, CLAMP)
            return (q_next, p_next)
        drive_tbn = jnp.swapaxes(input_drive_seq, 0, 1)

        def scan_fn(carry, drive):
            q, p = carry
            q, p = _rk4_step(q, p, drive, coupling, bias)
            return ((q, p), q)
        (_, _), q_trace_tbn = jax.lax.scan(scan_fn, (q0, p0), drive_tbn)
        return jnp.swapaxes(q_trace_tbn, 0, 1)

    def _L1_cond_ref(initial_state, inputs, W_ih, W_hh, b_ih, b_hh):
        import jax, jax.numpy as jnp
        import numpy as np
        B, T, D = (16, 128, 256)
        "ScanOverTime(GRU cell): sequential per-timestep module call with\n            dict-state passing; merge_dict_trees stacks the per-step\n            'state_predicted' tensors along axis=1 -> [B, T, D]."

        def cell(h, x):
            gi = x @ W_ih + b_ih
            gh = h @ W_hh + b_hh
            i_r, i_z, i_n = jnp.split(gi, 3, axis=-1)
            h_r, h_z, h_n = jnp.split(gh, 3, axis=-1)
            r = jax.nn.sigmoid(i_r + h_r)
            z = jax.nn.sigmoid(i_z + h_z)
            n = jnp.tanh(i_n + r * h_n)
            h_new = (1.0 - z) * n + z * h
            return (h_new, h_new)
        xs = jnp.swapaxes(inputs, 0, 1)
        _, hs = jax.lax.scan(cell, initial_state, xs)
        return jnp.swapaxes(hs, 0, 1)

    def _L2_cond_ref(input, grid, padding_mode, align_corners):
        import jax, jax.numpy as jnp
        import numpy as np
        N, C, L_IN, L_OUT = (32, 32, 256, 256)
        L = input.shape[2]
        if align_corners:
            ix = (grid + 1.0) * 0.5 * (L - 1)
        else:
            ix = ((grid + 1.0) * L - 1.0) * 0.5
        x0 = jnp.floor(ix)
        w1 = ix - x0
        w0 = 1.0 - w1
        i0 = x0.astype(jnp.int32)
        i1 = i0 + 1
        i0c = jnp.clip(i0, 0, L - 1)
        i1c = jnp.clip(i1, 0, L - 1)
        v0 = jnp.take_along_axis(input, i0c[:, None, :], axis=2)
        v1 = jnp.take_along_axis(input, i1c[:, None, :], axis=2)
        if padding_mode:
            return w0[:, None, :] * v0 + w1[:, None, :] * v1
        else:
            m0 = ((i0 >= 0) & (i0 < L)).astype(input.dtype)
            m1 = ((i1 >= 0) & (i1 < L)).astype(input.dtype)
            return (w0 * m0)[:, None, :] * v0 + (w1 * m1)[:, None, :] * v1

    def _L3_cond_ref(inputs, layer_idx, rms_weight, query_vectors, Wk, Wo, ln_gamma, ln_beta):
        import jax, jax.numpy as jnp
        import numpy as np
        NUM_BLOCKS = 8
        NUM_LAYERS = 4
        EPS = 1e-06
        B, S, H = inputs.shape
        block_size = max(1, S // NUM_BLOCKS)
        n_blocks = S // block_size
        block_repr = inputs.reshape(B, n_blocks, block_size, H).sum(axis=2)
        keys = jnp.einsum('bnh,kh->bnk', block_repr, Wk)
        rms = jnp.sqrt(jnp.mean(keys * keys, axis=-1, keepdims=True) + EPS)
        keys = keys / rms * rms_weight
        q = query_vectors[layer_idx]
        scores = jnp.einsum('bnh,h->bn', keys, q)
        attn = jax.nn.softmax(scores, axis=-1)
        attended = jnp.einsum('bn,bnh->bh', attn, block_repr)
        attended = jnp.broadcast_to(attended[:, None, :], (B, S, H))
        proj = jnp.einsum('bsh,kh->bsk', attended, Wo)
        x = inputs + proj
        mu = jnp.mean(x, axis=-1, keepdims=True)
        var = jnp.mean((x - mu) ** 2, axis=-1, keepdims=True)
        out = (x - mu) / jnp.sqrt(var + EPS) * ln_gamma + ln_beta
        return out
    x = x + _L0_cond_ref(cond_2048, cond_2048, x, L0_cond_coupling, L0_cond_bias)
    x = x + _L1_cond_ref(cond_2048, x, L1_cond_W_ih, L1_cond_W_hh, L1_cond_b_ih, L1_cond_b_hh)
    x = x + _L2_cond_ref(x, cond_2048, 1, 1)
    x = x + _L3_cond_ref(x, 1, L3_cond_rms_weight, cond_2048, L3_cond_Wk, L3_cond_Wo, L3_cond_ln_gamma, L3_cond_ln_beta)
    return x

_drawn_inputs = setup_inputs


def setup_inputs(seed=0):
    import zlib

    import numpy as np

    out = dict(_drawn_inputs(seed))
    spreads = {'L0_cond_bias': (0.0, 0.466),
     'L1_cond_b_ih': (0.0, 0.1),
     'L1_cond_b_hh': (0.0, 0.308),
     'L3_cond_rms_weight': (1.0, 0.2),
     'L3_cond_ln_gamma': (1.0, 0.2),
     'L3_cond_ln_beta': (0.0, 0.1)}
    factors = {'L0_cond_coupling': 3.028}
    for name, (base, spread) in spreads.items():
        noise = np.random.default_rng([zlib.crc32(name.encode()), seed]).standard_normal(out[name].shape)
        drawn = base * np.exp(spread * noise) if base else spread * noise
        out[name] = jnp.asarray(drawn.astype(out[name].dtype))
    for name, factor in factors.items():
        out[name] = (out[name] * factor).astype(out[name].dtype)
    return out
```

```python
from contextlib import ExitStack

import numpy as np

import concourse.bass as bass
from concourse import mybir

F32 = mybir.dt.float32
BF16 = mybir.dt.bfloat16
F16 = mybir.dt.float16
I32 = mybir.dt.int32
ALU = mybir.AluOpType
ACT = mybir.ActivationFunctionType
AX_X = mybir.AxisListType.X

P = 128
B, T, N = 32, 32, 256
R = N // P
J = 4
W = R * B
TILES = T // 4
PEEL, BODY = 4, 4
NBLK = 8
EPS = 1e-6

DT, EPSN, ALPHA, BETA, CLAMP = 0.01, 0.08, 0.7, 0.8, 20.0
C = 0.5 * DT
SHIFT = ALPHA / BETA


def stage_coefficients():
    e = np.eye(5)
    p, q1, q2, q3, q4 = e
    a = EPSN * C
    p2 = p + a * (q1 - BETA * p)
    p3 = p + a * (q2 - BETA * p2)
    p4 = p + 2 * a * (q3 - BETA * p3)
    pn = p + a / 3 * ((q1 - BETA * p) + 2 * (q2 - BETA * p2) + 2 * (q3 - BETA * p3) + (q4 - BETA * p4))
    l3 = q1 - C * p2
    l4 = (q1 - 2 * C * p3) / 2
    lf = (-q1 + q2 + 2 * q3 + q4) / 3 - C / 3 * p4
    return l3, l4, lf, pn


L3C, L4C, LFC, PNC = (tuple(float(v) for v in x) for x in stage_coefficients())
PU = 2 * PNC[4]

K_ID, K_FEAT, K_IND, K_BD, K_HALF, K_END = 0, 128, 130, 162, 178, 182


def constants():
    k = np.zeros((P, K_END), np.float32)
    k[:, K_ID:K_ID + P] = np.eye(P)
    p = np.arange(P)
    for r in range(R):
        k[:, K_FEAT + r] = -(P * r + p)
    k[p, K_IND + (p // T) * NBLK + (p % T) // (T // NBLK)] = 1
    k[p, K_BD + p // NBLK] = 1
    k[:, K_HALF:K_HALF + 4] = -0.5
    sel = np.zeros((96, TILES, P), np.float32)
    for part in range(3):
        for g in range(TILES):
            for b4 in range(4):
                sel[32 * part + 4 * g + b4, g, T * b4:T * b4 + T] = 1
    bsel = np.zeros((P, P), np.float32)
    for part in range(3):
        for j in range(J):
            for s in range(2):
                bsel[32 * part + 2 * j + s, 32 * j:32 * j + 32] = 1
    return k, sel.reshape(96, TILES * P), bsel


def build(nc, x, cond, coupling, l0_bias, w_ih, w_hh, b_ih, b_hh, rms_w, wk, wo, gamma, beta, konst, ksel, kbsel, out):
    with ExitStack() as ctx:
        def sb(name, shape, dt=F32):
            return ctx.enter_context(nc.sbuf_tensor(name, shape, dt))

        def ps(name, shape, dt=F32):
            return ctx.enter_context(nc.psum_tensor(name, shape, dt))

        def sem(name):
            return ctx.enter_context(nc.semaphore(name))

        kon = sb("kon", [P, K_END])
        selw = sb("selw", [96, TILES, P])
        selb = sb("selb", [96, TILES, P], BF16)
        bselw = sb("bselw", [P, P])
        bselb = sb("bselb", [P, P], BF16)
        coup = sb("coup", [P, R, N])
        cmax = sb("cmax", [P, 1])
        cmax1 = sb("cmax1", [1, 4])
        ones = sb("ones", [1, P])
        unit = sb("unit", [P, 4])
        w_hi = sb("w_hi", [P, R, R, P], F16)
        w_lo = sb("w_lo", [P, R, R, P], F16)
        condn = sb("condn", [B + 1, N])
        condT = sb("condT", [P, W])
        xn = sb("xn", [P, TILES, N])
        xT = sb("xT", [P, T, W])
        drv = sb("drv", [P, T, W])
        drv3 = sb("drv3", [P, T, W])
        lb = sb("lb", [P, R])
        dbias = sb("dbias", [P, R])
        q1raw = sb("q1raw", [P, W])
        q1 = sb("q1", [P, W])
        q2 = sb("q2", [P, W])
        q3 = sb("q3", [P, W])
        q4h = sb("q4h", [P, W])
        pu = sb("pu", [P, W])
        pn = sb("pn", [P, 2, W])
        psum_acc = sb("pacc", [P, 3, W])
        t_hi = sb("t_hi", [P, W], F16)
        t_lo = sb("t_lo", [P, W], F16)
        t_full = sb("t_full", [P, W])
        sq = sb("sq", [P, W])
        g3 = sb("g3", [P, W])
        base = sb("base", [P, W])
        gp = sb("gp", [P, 3, W])
        gpf = sb("gpf", [P, W])
        z = sb("z", [P, 3, W])
        zf = sb("zf", [P, W])
        lin2 = sb("lin2", [P, W])
        lin3 = sb("lin3", [P, W])
        lin4 = sb("lin4", [P, 2, W])
        linf = sb("linf", [P, 4, W])
        wih = sb("wih", [P, R, 3, N])
        whh = sb("whh", [P, R, 3, N])
        bsrc = sb("bsrc", [P, 4, 64])
        bres = sb("bres", [8, 2, N])
        bprt = sb("bprt", [8, 2, N], BF16)
        bmov = sb("bmov", [P, N], BF16)
        x1 = sb("x1", [P, 2, W])
        hT = sb("hT", [P, W])
        hB = sb("hB", [P, W])
        rz = sb("rz", [P, 2, 64])
        zg = sb("zg", [P, 64])
        rn = sb("rn", [P, 64])
        pre = sb("pre", [P, 64])
        ng = sb("ng", [P, 64])
        un = sb("un", [P, 64])
        zh = sb("zh", [P, 64])
        x2 = sb("x2", [P, R, B, T])
        gridn = sb("gridn", [P, 64])
        gridx = sb("gridx", [P, 64])
        ixb = sb("ixb", [P, B * N])
        dist = sb("dist", [P, R, N])
        hat = sb("hat", [P, B * R * N])
        wkn = sb("wkn", [P, 2, N])
        won = sb("won", [P, 2, N])
        wkT = sb("wkT", [P, 2, N])
        woT = sb("woT", [P, 2, N])
        rmsb = sb("rmsb", [P, N])
        qvb = sb("qvb", [P, N])
        qk = sb("qk", [P, N])
        gam = sb("gam", [P, N])
        bet = sb("bet", [P, N])
        x3 = xn
        x3b = drv[:, :, :].rearrange("p t w -> p (t w)").rearrange("p (g n) -> p g n", g=TILES)
        blk = sb("blk", [P, 2, N])
        blkT = sb("blkT", [P, 2, 2, P])
        junk = sb("junk", [P, 4, N])
        ss = sb("ss", [P, 2])
        sc = sb("sc", [P, 2])
        rs = sb("rs", [P, 2])
        score = sb("score", [P, 2])
        sm = sb("sm", [2, P])
        ex = sb("ex", [2, P])
        att = sb("att", [2, P])
        mx = sb("mx", [2, 3, 16])
        attb = sb("attb", [P, 2, 16])
        attT = sb("attT", [P, 2, B])
        prj = sb("prj", [96, N], BF16)
        prt = sb("prt", [B, N])
        prm = sb("prm", [B, N], BF16)
        st6 = sb("st6", [P, TILES, 6])
        mv = sb("mv", [P, TILES, 2])
        rstd = sb("rstd", [P, TILES])
        nrm = sb("nrm", [P, 2, N])
        yout = drv3[:, :, :].rearrange("p t w -> p (t w)").rearrange("p (g n) -> p g n", g=TILES)

        p_l0 = ps("p_l0", [P, 512])
        p_gru = [ps(f"p_gru{i}", [P, 512]) for i in range(2)]
        p_x = ps("p_x", [P, 512])
        p_x3 = ps("p_x3", [P, TILES, N])

        scratch = nc.dram_tensor("grid_scratch", [B, N], F32, kind="Internal").ap()

        ident = kon[:, K_ID:K_ID + P]

        ld_coup, ld_cond, ld_kon, ld_hb = sem("ld_coup"), sem("ld_cond"), sem("ld_kon"), sem("ld_hb")
        ld_grid, ld_ih, ld_hh, ld_bias, ld_att, ld_kb = sem("ld_grid"), sem("ld_ih"), sem("ld_hh"), sem("ld_bias"), sem("ld_att"), sem("ld_kb")
        ld_x = [sem(f"ld_x{i}") for i in range(TILES)]
        ld_ix = sem("ld_ix")
        zeroed, grid_ready, grid_out = sem("zeroed"), sem("grid_ready"), sem("grid_out")
        cmax_ready, cmax_row, cmax_red, unit_psum, unit_ready, unit_step = (
            sem("cmax_ready"), sem("cmax_row"), sem("cmax_red"), sem("unit_psum"), sem("unit_ready"), sem("unit_step"))
        coupT_psum, w_hi_ready, w_ready, condT_psum, start_ready = (
            sem("coupT_psum"), sem("w_hi_ready"), sem("w_ready"), sem("condT_psum"), sem("start_ready"))
        xT_psum, xT_ready, dbias_ready, drv_ready = sem("xT_psum"), sem("xT_ready"), sem("dbias_ready"), sem("drv_ready")
        bias_step, bias_ready, kb_ready, qk_ready = sem("bias_step"), sem("bias_ready"), sem("kb_ready"), sem("qk_ready")
        q_ready, clipped, t_hi_ready, t_ready, t_lo_ready = (
            sem("q_ready"), sem("clipped"), sem("t_hi_ready"), sem("t_ready"), sem("t_lo_ready"))
        sq_ready, g3_ready, base_ready, coupled = sem("sq_ready"), sem("g3_ready"), sem("base_ready"), sem("coupled")
        lin_done, p_ready = sem("lin_done"), sem("p_ready")
        sp2_ready, sp34_ready, spf_ready = sem("sp2_ready"), sem("sp34_ready"), sem("spf_ready")
        z2_ready, z34_ready, zf_ready, lin2_ready = sem("z2_ready"), sem("z34_ready"), sem("zf_ready"), sem("lin2_ready")
        x1_ready, x2_ready, zh_ready = sem("x1_ready"), sem("x2_ready"), sem("zh_ready")
        gate_psum, rz_ready, zg_ready, n_ready = sem("gate_psum"), sem("rz_ready"), sem("zg_ready"), sem("n_ready")
        rn_ready, pre_ready, un_ready, hB_ready, hT_ready = (
            sem("rn_ready"), sem("pre_ready"), sem("un_ready"), sem("hB_ready"), sem("hT_ready"))
        dist_ready, hat_ready = sem("dist_ready"), sem("hat_ready")
        wT_psum, wT_ready = sem("wT_psum"), sem("wT_ready")
        x3_psum, x3_act, x3_dve, x3b_ready = sem("x3_psum"), sem("x3_act"), sem("x3_dve"), sem("x3b_ready")
        blk_psum, blk_ready, blkT_psum, blkT_ready = sem("blk_psum"), sem("blk_ready"), sem("blkT_psum"), sem("blkT_ready")
        key_psum, ss_ready, sc_ready, ms_ready, rs_ready, score_ready = (
            sem("key_psum"), sem("ss_ready"), sem("sc_ready"), sem("ms_ready"), sem("rs_ready"), sem("score_ready"))
        scoreT_psum, soft_step, exp_ready, att_ready, attc_psum, attb_ready = (
            sem("scoreT_psum"), sem("soft_step"), sem("exp_ready"), sem("att_ready"), sem("attc_psum"), sem("attb_ready"))
        attT_psum, attT_ready, prj_psum, prj_step, prj_ready, y_psum = (
            sem("attT_psum"), sem("attT_ready"), sem("prj_psum"), sem("prj_step"), sem("prj_ready"), sem("y_psum"))
        stat_done, var_ready, rstd_ready, nrm_ready, y_ready, stored = (
            sem("stat_done"), sem("var_ready"), sem("rstd_ready"), sem("nrm_ready"), sem("y_ready"), sem("stored"))

        LIN = ["pa", "l3", "pb", "l4a", "l4b", "lfa", "lfb", "lfc", "pc", "lf", "pd"]

        def lin_count(t, name):
            return len(LIN) * t + LIN.index(name) + 1

        q_of = {1: q1, 2: q2, 3: q3, 4: q4h}

        block = ctx.enter_context(nc.Block())

        @block.sync
        def _(sp):
            for r in range(R):
                sp.dma_start(coup[:, r, :], coupling[P * r:P * r + P, :]).then_inc(ld_coup, 16)
            sp.dma_start(condn[0:B, :], cond).then_inc(ld_cond, 16)
            sp.dma_start(condn[B:B + 1, :], l0_bias.rearrange("(o n) -> o n", o=1)).then_inc(ld_cond, 16)
            sp.dma_start(gridn[:, :], cond.rearrange("b (q f) -> (b q) f", f=64)).then_inc(ld_grid, 16)
            for g in range(TILES):
                for tt in range(4):
                    sp.dma_start(xn[32 * tt:32 * tt + 32, g, :], x[:, 4 * g + tt, :]).then_inc(ld_x[g], 16)
                if g == 1:
                    sp.dma_start(whh[:, :, :, :].rearrange("p r g n -> p r (g n)"),
                                 w_hh.rearrange("(r p) m -> p r m", r=R)).then_inc(ld_hh, 16)
            sp.wait_ge(grid_ready, 1)
            sp.dma_start(scratch.rearrange("b (q f) -> (b q) f", f=64), gridx[:, :]).then_inc(grid_out, 16)
            sp.wait_ge(grid_out, 16)
            flat = scratch.rearrange("b n -> (b n)")
            for h in range(4):
                seg = B * N // 4
                sp.dma_start(ixb[:, seg * h:seg * (h + 1)],
                             flat[seg * h:seg * (h + 1)].partition_broadcast(P)).then_inc(ld_ix, 16)
            sp.dma_start(wkn[:, :, :], wk.rearrange("(c p) h -> p c h", p=P)).then_inc(ld_att, 16)
            sp.dma_start(won[:, :, :], wo.rearrange("(c p) h -> p c h", p=P)).then_inc(ld_att, 16)
            sp.dma_start(rmsb[:, :], rms_w.partition_broadcast(P)).then_inc(ld_att, 16)
            sp.dma_start(gam[:, :], gamma.partition_broadcast(P)).then_inc(ld_att, 16)
            sp.dma_start(bet[:, :], beta.partition_broadcast(P)).then_inc(ld_att, 16)
            sp.dma_start(qvb[:, :], cond[1, :].partition_broadcast(P)).then_inc(ld_att, 16)
            for g in range(TILES):
                sp.wait_ge(y_ready, g + 1)
                sp.dma_start(out[4 * g:4 * g + 4, :, :].rearrange("b t n -> (b t) n"), yout[:, g, :]).then_inc(stored, 16)
            sp.wait_ge(stored, 16 * TILES)

        @block.scalar
        def _(act):
            act.dma_start(kon[:, :], konst).then_inc(ld_kon, 16)
            for j in range(J):
                act.dma_start(hB[32 * j:32 * j + 32, :].rearrange("b (r i) -> b r i", r=R),
                              cond.rearrange("b (r k i) -> k b r i", r=R, k=J)[j]).then_inc(ld_hb, 16)
            rows = w_ih.rearrange("(r p) m -> p r m", r=R)
            act.dma_start(wih[:, :, 0, :], rows[:, :, 2 * N:3 * N]).then_inc(ld_ih, 16)
            act.dma_start(wih[:, :, 1:3, :].rearrange("p r g n -> p r (g n)"), rows[:, :, 0:2 * N]).then_inc(ld_ih, 16)
            act.dma_start(bselw[:, :], kbsel).then_inc(ld_kb, 16)
            act.dma_start(selw[:, :, :].rearrange("p g m -> p (g m)"), ksel).then_inc(ld_kb, 16)
            act.wait_ge(zeroed, 1)
            bi = b_ih.rearrange("(g r j i) -> j g r i", g=3, r=R, j=J)
            bh = b_hh.rearrange("(g r j i) -> j (g r) i", g=3, r=R, j=J)
            bd = bsrc[:, :, :].rearrange("p g (r i) -> p g r i", r=R)
            act.dma_start(bd[0:8:2, 0, :, :], bi[:, 2, :, :]).then_inc(ld_bias, 16)
            act.dma_start(bd[0:8:2, 1:3, :, :], bi[:, 0:2, :, :]).then_inc(ld_bias, 16)
            act.dma_start(bd[1:8:2, 1:4, :, :].rearrange("p g r i -> p (g r) i"), bh).then_inc(ld_bias, 16)

            act.wait_ge(condT_psum, 1)
            cp = p_l0[:, 0:R * (B + 1)].rearrange("p (r b) -> p r b", r=R)
            nc.scalar.copy(condT[:, :].rearrange("p (r b) -> p r b", r=R), cp[:, :, 0:B])
            nc.scalar.copy(lb[:, :].rearrange("p (r o) -> p r o", o=1), cp[:, :, B:B + 1]).then_inc(start_ready, 1)

            def x_tiles(first, count):
                act.wait_ge(xT_psum, (first + 1) // 2 + 1)
                src = p_x[:, 0:count * 2 * P].rearrange("p (g r t b) -> p g r (t b)", g=count, r=R, b=B)
                dst = xT[:, 4 * first:4 * (first + count), :].rearrange("p (g t) (r b) -> p g r t b", t=4, b=B)
                for g in range(count):
                    for r in range(R):
                        ins = nc.scalar.copy(dst[:, g, r, :, :], src[:, g, r, :].rearrange("p (t b) -> p t b", b=B))
                ins.then_inc(xT_ready, 1)

            def scale_p(t, which):
                act.wait_ge(p_ready, t + 1)
                if which == "f":
                    nc.scalar.mul(gpf[:, :], pu[:, :], -PU * LFC[0]).then_inc(spf_ready, 1)
                elif which == 2:
                    nc.scalar.mul(gp[:, 0, :], pu[:, :], PU * C).then_inc(sp2_ready, 1)
                else:
                    nc.scalar.mul(gp[:, 1, :], pu[:, :], -PU * L3C[0])
                    nc.scalar.mul(gp[:, 2, :], pu[:, :], -PU * L4C[0]).then_inc(sp34_ready, 1)

            def hat_dist(b, r):
                nc.scalar.activation(dist[:, r, :], ixb[:, bass.ds(b * N, N)], ACT.Abs,
                                     bias=kon[:, K_FEAT + r:K_FEAT + r + 1]).then_inc(dist_ready, 1)

            def hat_weight(b, r):
                act.wait_ge(dist_ready, b * R + (r + 1))
                nc.scalar.activation(hat[:, bass.ds(b * R * N + r * N, N)], dist[:, r, :], ACT.Relu,
                                     bias=1.0, scale=-1.0).then_inc(hat_ready, 1)

            def gate_rz(u):
                act.wait_ge(gate_psum, u + 1)
                nc.scalar.activation(rz[:, :, :].rearrange("p g f -> p (g f)"), p_gru[u_parity[0]][:, 64:192],
                                     ACT.Tanh, scale=0.5).then_inc(rz_ready, 1)
                act.wait_ge(rz_ready, u + 1)
                nc.scalar.activation(zg[:, :], rz[:, 1, :], ACT.Copy, bias=0.5, scale=0.5).then_inc(zg_ready, 1)

            def gate_n(u):
                act.wait_ge(pre_ready, u + 1)
                nc.scalar.activation(ng[:, :], pre[:, :], ACT.Tanh).then_inc(n_ready, 1)

            u_parity = [0]

            def step(t, k, network, gates, hats):
                u_parity[0] = k % 2
                for s in range(1, 5):
                    if network:
                        src = q1raw if s == 1 else q_of[s]
                        scale = 2.0 if s == 4 else 1.0
                        act.wait_ge(q_ready, t * 4 + s)
                        nc.scalar.activation(t_hi[:, :], src[:, :], ACT.Tanh, scale=scale).then_inc(t_hi_ready, 1)
                        nc.scalar.activation(t_full[:, :], src[:, :], ACT.Tanh, scale=scale).then_inc(t_ready, 1)
                        if s == 1:
                            act.wait_ge(clipped, t + 1)
                        nc.scalar.activation(sq[:, :], q_of[s][:, :], ACT.Square, scale=scale).then_inc(sq_ready, 1)
                    if s == 1:
                        if gates:
                            gate_rz(t - 2)
                        if network:
                            scale_p(t, "f")
                        if hats:
                            hat_dist(t - PEEL, 0)
                        if k == 0 and network:
                            x_tiles(1, 2)
                    if s == 2:
                        if gates:
                            gate_n(t - 2)
                        if hats:
                            hat_weight(t - PEEL, 0)
                        if k == 0 and network:
                            x_tiles(3, 2)
                    if s == 3:
                        if hats:
                            hat_dist(t - PEEL, 1)
                            hat_weight(t - PEEL, 1)
                        if k == 0 and network:
                            x_tiles(5, 2)
                    if s == 4:
                        if k == 0 and network:
                            x_tiles(7, 1)
                        if network and k != T - 1:
                            scale_p(t + 1, 2)
                            scale_p(t + 1, 34)

            x_tiles(0, 1)
            scale_p(0, 2)
            scale_p(0, 34)
            for t in range(PEEL):
                step(t, t, True, t >= 2, False)
            act.wait_ge(ld_ix, 16 * 4)
            for k in range(PEEL, T - BODY):
                step(k, k, True, True, True)
            for k in range(T - BODY, T):
                step(k, k, True, True, True)
            for b in range(T - PEEL, T):
                for r in range(R):
                    hat_dist(b, r)
                    hat_weight(b, r)
                if b == T - PEEL:
                    step(T, T, False, True, False)
                if b == T - PEEL + 1:
                    step(T + 1, T + 1, False, True, False)
            act.wait_ge(wT_psum, 1)
            nc.scalar.copy(wkT[:, :, :].rearrange("p c n -> p (c n)"), p_x[:, :]).then_inc(wT_ready, 1)
            act.wait_ge(wT_psum, 2)
            nc.scalar.copy(woT[:, :, :].rearrange("p c n -> p (c n)"), p_l0[:, :]).then_inc(wT_ready, 1)
            for m in (0, 2):
                act.wait_ge(x3_psum, m + 1)
                nc.scalar.copy(x3[:, 2 * m:2 * m + 2, :], p_x3[:, 2 * m:2 * m + 2, :]).then_inc(x3_act, 1)
            act.wait_ge(blkT_psum, 1)
            nc.scalar.copy(blkT[:, :, :, :].rearrange("p c h n -> p (c h n)"), p_l0[:, :]).then_inc(blkT_ready, 1)
            act.wait_ge(key_psum, 1)
            nc.scalar.activation(junk[:, 0, :], p_gru[0][:, 0:N], ACT.Square, accum_out=ss[:, 0:1]).then_inc(ss_ready, 1)
            act.wait_ge(sc_ready, 1)
            nc.scalar.activation(junk[:, 3, :], p_gru[1][:, 0:N], ACT.Square, accum_out=ss[:, 1:2]).then_inc(ss_ready, 1)
            act.wait_ge(soft_step, 2)
            nc.scalar.activation(ex[:, :], sm[:, :], ACT.Exp).then_inc(exp_ready, 1)

        @block.tensor
        def _(pe):
            pe.wait_ge(ld_coup, 16 * R)
            pe.wait_ge(ld_kon, 16)
            for rm in range(R):
                for rnn in range(R):
                    c0 = (rm * R + rnn) * P
                    ins = nc.tensor.transpose(p_gru[0][:, c0:c0 + P], coup[:, rnn, P * rm:P * rm + P], ident)
            ins.then_inc(coupT_psum, 1)
            pe.wait_ge(ld_cond, 32)
            for r in range(R):
                ins = nc.tensor.transpose(p_l0[:, (B + 1) * r:(B + 1) * (r + 1)], condn[:, P * r:P * r + P], kon[0:B + 1, K_ID:K_ID + B + 1])
            ins.then_inc(condT_psum, 1)

            def x_tiles(first, count):
                for g in range(first, first + count):
                    pe.wait_ge(ld_x[g], 64)
                if first:
                    pe.wait_ge(xT_ready, (first + 1) // 2)
                for g in range(first, first + count):
                    for r in range(R):
                        c0 = ((g - first) * R + r) * P
                        ins = nc.tensor.transpose(p_x[:, c0:c0 + P], xn[:, g, P * r:P * r + P], ident)
                ins.then_inc(xT_psum, 1)

            x_tiles(0, 1)
            pe.wait_ge(cmax_ready, 1)
            nc.tensor.transpose(p_gru[1][0:1, 0:P], cmax[:, :], ident).then_inc(cmax_row, 1)
            pe.wait_ge(cmax_red, 1)
            nc.tensor.matmul(p_gru[1][:, P:P + 1], ones[:, :], cmax1[:, 2:3], start=True, stop=True).then_inc(unit_psum, 1)
            pe.wait_ge(w_ready, 1)

            def couple(w, tt, first, last):
                for rnn in range(R):
                    for rm in range(R):
                        ins = nc.tensor.matmul(p_l0[:, 32 * rnn:32 * rnn + 32], w[:, rm, rnn, :], tt[:, 32 * rm:32 * rm + 32],
                                               start=first and rnn == 0 and rm == 0, stop=last and rm == R - 1,
                                               skip_group_check=True)
                return ins

            def gate_bias(par):
                nc.tensor.matmul(p_gru[par][:, 0:N], bselb[:, :], bmov[:, :], start=True, stop=False, skip_group_check=True)

            def gate_x(par, r):
                for j in range(J):
                    nc.tensor.matmul(p_gru[par][32 * j:32 * j + 32, 0:192], x1[:, par, 32 * r:32 * r + 32],
                                     wih[:, r, :, :].rearrange("p g (q i) -> p g q i", q=R)[:, :, :, 32 * j:32 * j + 32], start=False, stop=False, skip_group_check=True)

            def gate_h(par, r):
                for j in range(J):
                    ins = nc.tensor.matmul(p_gru[par][32 * j:32 * j + 32, 64:256], hT[:, 32 * r:32 * r + 32],
                                           whh[:, r, :, :].rearrange("p g (q i) -> p g q i", q=R)[:, :, :, 32 * j:32 * j + 32], start=False, stop=(r == R - 1),
                                           skip_group_check=True)
                if r == R - 1:
                    ins.then_inc(gate_psum, 1)

            def step(t, k, network, products):
                par = (k - 1) % 2
                for s in range(1, 5):
                    if network:
                        pe.wait_ge(t_hi_ready, t * 4 + s)
                        couple(w_hi, t_hi, True, False)
                        couple(w_lo, t_hi, False, False)
                    if s == 1 and products:
                        if k == 1:
                            pe.wait_ge(bias_ready, 1)
                            pe.wait_ge(kb_ready, 1)
                        gate_bias(par)
                    if network:
                        pe.wait_ge(t_lo_ready, t * 4 + s)
                        couple(w_hi, t_lo, False, True).then_inc(coupled, 1)
                    if products:
                        if s == 1:
                            if k == 1:
                                pe.wait_ge(ld_ih, 16 * 2)
                            pe.wait_ge(x1_ready, t)
                            gate_x(par, 0)
                        if s == 2:
                            gate_x(par, 1)
                        if s == 3:
                            if k == 1:
                                pe.wait_ge(ld_hh, 16)
                            pe.wait_ge(hT_ready, t)
                            gate_h(par, 0)
                        if s == 4:
                            gate_h(par, 1)
                    if k == 0 and network:
                        x_tiles(2 * s - 1, 2 if s < 4 else 1)

            for t in range(PEEL):
                step(t, t, True, t >= 1)
            for k in range(PEEL, T - BODY):
                step(k, k, True, True)
            for k in range(T - BODY, T):
                step(k, k, True, True)
            step(T, T, False, True)

            pe.wait_ge(ld_att, 16 * 6)
            pe.wait_ge(xT_ready, 5)
            for n, (src, dst) in enumerate(((wkn, p_x), (won, p_l0))):
                if n == 1:
                    pe.wait_ge(q_ready, 4 * T + 1)
                for ch in range(2):
                    for ck in range(2):
                        c0 = ch * N + ck * P
                        ins = nc.tensor.transpose(dst[:, c0:c0 + P], src[:, ck, P * ch:P * ch + P], ident)
                ins.then_inc(wT_psum, 1)

            pe.wait_ge(x2_ready, T)
            for g in range(TILES):
                pe.wait_ge(hat_ready, (4 * g + 4) * R)
                for r in range(R):
                    for j in range(J):
                        b = 4 * g + j
                        nc.tensor.matmul(p_x3[32 * j:32 * j + 32, g, :], x2[:, r, b, :],
                                         hat[:, (b * R + r) * N:(b * R + r + 1) * N],
                                         start=(r == 0 and g % 2 == 0), stop=False, skip_group_check=True)
                    for j in range(J):
                        ins = nc.tensor.matmul(p_x3[32 * j:32 * j + 32, g, P * r:P * r + P], x2[:, r, 4 * g + j, :], ident,
                                               start=False, stop=(r == R - 1), skip_group_check=True)
                if g % 2:
                    ins.then_inc(x3_psum, 1)

            pe.wait_ge(wT_ready, 2)
            for g in range(TILES):
                m = g // 2
                pe.wait_ge(x3_dve if m % 2 else x3_act, m // 2 + 1)
                j, half = g % 4, g // 4
                ins = nc.tensor.matmul(p_x[32 * j:32 * j + 32, half * N:half * N + N], kon[:, K_IND:K_IND + 32],
                                       x3[:, g, :], start=True, stop=True, skip_group_check=True)
            ins.then_inc(blk_psum, 1)
            pe.wait_ge(blk_ready, 1)
            for c in range(2):
                for half in range(2):
                    c0 = (c * 2 + half) * P
                    ins = nc.tensor.transpose(p_l0[:, c0:c0 + P], blk[:, half, P * c:P * c + P], ident)
            ins.then_inc(blkT_psum, 1)
            pe.wait_ge(blkT_ready, 1)
            for half in range(2):
                for c in range(2):
                    ins = nc.tensor.matmul(p_gru[half][:, 0:N], blkT[:, c, half, :], wkT[:, c, :], start=(c == 0), stop=(c == 1))
            ins.then_inc(key_psum, 1)
            pe.wait_ge(score_ready, 1)
            nc.tensor.transpose(p_gru[0][0:2, 0:P], score[:, :], ident).then_inc(scoreT_psum, 1)
            pe.wait_ge(att_ready, 1)
            nc.tensor.transpose(p_gru[1][:, 0:2], att[:, :], kon[0:2, K_ID:K_ID + 2]).then_inc(attc_psum, 1)
            pe.wait_ge(attb_ready, 1)
            for c in range(2):
                for half in range(2):
                    c0 = c * B + half * 16
                    ins = nc.tensor.matmul(p_l0[:, c0:c0 + 16], blk[:, half, P * c:P * c + P], attb[:, half, :],
                                           start=(c == 0 and half == 0), stop=True, skip_group_check=True)
            ins.then_inc(attT_psum, 1)
            pe.wait_ge(attT_ready, 1)
            for c in range(2):
                ins = nc.tensor.matmul(p_x[0:B, 0:N], attT[:, c, :], woT[:, c, :], start=(c == 0), stop=(c == 1))
            ins.then_inc(prj_psum, 1)
            pe.wait_ge(prj_ready, 1)
            for g in range(TILES):
                ins = nc.tensor.matmul(p_x3[:, g, :], selb[:, g, :], prj[:, :], start=False, stop=True, skip_group_check=True)
                if g % 2:
                    ins.then_inc(y_psum, 1)

        @block.gpsimd
        def _(pool):
            nc.gpsimd.memset(bsrc[:, :, :], 0.0).then_inc(zeroed, 1)
            nc.gpsimd.memset(bmov[:, :], 0.0).then_inc(bias_step, 1)
            pool.wait_ge(ld_grid, 16)
            nc.gpsimd.tensor_scalar(gridn[:, :], gridn[:, :], 1.0, 0.5 * (N - 1), ALU.add, ALU.mult).then_inc(bias_step, 1)
            pool.wait_ge(bias_step, 2)
            nc.gpsimd.tensor_scalar(gridx[:, :], gridn[:, :], 0.0, float(N - 1), ALU.max, ALU.min).then_inc(grid_ready, 1)
            pool.wait_ge(start_ready, 1)
            nc.gpsimd.tensor_scalar(pu[:, :], condT[:, :], -SHIFT, 1.0 / PU, ALU.add, ALU.mult).then_inc(p_ready, 1)
            nc.gpsimd.tensor_scalar(dbias[:, :], lb[:, :], -SHIFT, C, ALU.add, ALU.mult).then_inc(dbias_ready, 1)
            pool.wait_ge(dbias_ready, 1)

            def drive(first, count, n):
                pool.wait_ge(xT_ready, n)
                a, b = 4 * first, 4 * (first + count)
                for r in range(R):
                    ins = nc.gpsimd.tensor_scalar(drv[:, a:b, 32 * r:32 * r + 32], xT[:, a:b, 32 * r:32 * r + 32],
                                                  C, dbias[:, r:r + 1], ALU.mult, ALU.add)
                ins.then_inc(drv_ready, 1)
                pool.wait_ge(drv_ready, n)
                nc.gpsimd.tensor_scalar(drv3[:, a:b, :], drv[:, a:b, :], 1.0 / 3.0, None, ALU.mult)

            def z2(t):
                pool.wait_ge(sp2_ready, t + 1)
                nc.gpsimd.tensor_tensor(z[:, 0:1, :], drv[:, bass.ds(t, 1), :], gp[:, 0:1, :], ALU.subtract).then_inc(z2_ready, 1)

            def step(t, k, network, inputs, gates):
                if network:
                    pool.wait_ge(sp34_ready, t + 1)
                    for n in (1, 2):
                        ins = nc.gpsimd.tensor_tensor(z[:, n:n + 1, :], drv[:, bass.ds(t, 1), :], gp[:, n:n + 1, :], ALU.subtract)
                    ins.then_inc(z34_ready, 1)
                pool.wait_ge(clipped, t + 1)
                if network:
                    pool.wait_ge(z2_ready, t + 1)
                    nc.gpsimd.tensor_tensor(lin2[:, :], z[:, 0, :], q1[:, :], ALU.add).then_inc(lin2_ready, 1)
                if inputs:
                    if not network:
                        pool.wait_ge(x2_ready, t - 2)
                    nc.gpsimd.tensor_tensor(x1[:, (k - 1) % 2:(k - 1) % 2 + 1, :], xT[:, bass.ds(t - 1, 1), :],
                                            q1[:, :].rearrange("p (o w) -> p o w", o=1), ALU.add).then_inc(x1_ready, 1)
                if network:
                    pool.wait_ge(spf_ready, t + 1)
                    nc.gpsimd.tensor_tensor(zf[:, :].rearrange("p (o w) -> p o w", o=1), drv3[:, bass.ds(t, 1), :],
                                            gpf[:, :].rearrange("p (o w) -> p o w", o=1), ALU.subtract).then_inc(zf_ready, 1)
                if k == 0 and network:
                    drive(1, 2, 2)
                    drive(3, 2, 3)
                    drive(5, 2, 4)
                if gates:
                    mix(t, k)
                if network:
                    pool.wait_ge(lin_done, t * len(LIN) + len(LIN))
                    nc.gpsimd.tensor_scalar(pu[:, :], pn[:, 1, :], (-CLAMP - SHIFT) / PU, (CLAMP - SHIFT) / PU,
                                            ALU.max, ALU.min).then_inc(p_ready, 1)
                    if k == 0:
                        drive(7, 1, 5)
                    if k != T - 1:
                        z2(t + 1)

            def mix(t, k):
                pool.wait_ge(zg_ready, t - 1)
                if k == 2:
                    pool.wait_ge(ld_hb, 16 * J)
                else:
                    pool.wait_ge(hB_ready, t - 2)
                nc.gpsimd.tensor_tensor(zh[:, :], zg[:, :], hB[:, :], ALU.mult).then_inc(zh_ready, 1)
                pool.wait_ge(hT_ready, t)
                nc.gpsimd.tensor_tensor(x2[:, :, :, bass.ds(t - 2, 1)],
                                        x1[:, k % 2, :].rearrange("p (r b o) -> p r b o", r=R, o=1),
                                        hT[:, :].rearrange("p (r b o) -> p r b o", r=R, o=1), ALU.add).then_inc(x2_ready, 1)

            drive(0, 1, 1)
            z2(0)
            for t in range(PEEL):
                step(t, t, True, t >= 1, t >= 2)
                if t == 0:
                    pool.wait_ge(ld_bias, 48)
                    rows = bsrc[0:8, :, :].rearrange("p g f -> p (g f)")
                    nc.gpsimd.tensor_copy(bmov[0:8, :], rows).then_inc(bias_step, 1)
                    pool.wait_ge(bias_step, 3)
                    nc.gpsimd.tensor_tensor(bres[:, 0, :], rows, bmov[0:8, :], ALU.subtract).then_inc(bias_step, 1)
                    pool.wait_ge(bias_step, 4)
                    nc.gpsimd.tensor_copy(bprt[:, 0, :], bres[:, 0, :]).then_inc(bias_step, 1)
                    nc.gpsimd.tensor_copy(bmov[32:40, :], bres[:, 0, :]).then_inc(bias_step, 1)
                    pool.wait_ge(bias_step, 6)
                    nc.gpsimd.tensor_tensor(bmov[64:72, :], bres[:, 0, :], bprt[:, 0, :], ALU.subtract).then_inc(bias_ready, 1)
                    pool.wait_ge(bias_ready, 1)
                    pool.wait_ge(ld_kb, 32)
                    nc.gpsimd.tensor_copy(bselb[:, :], bselw[:, :]).then_inc(kb_ready, 1)
                    nc.gpsimd.tensor_copy(selb[:, :, :], selw[:, :, :])
            for k in range(PEEL, T - BODY):
                step(k, k, True, True, True)
            for k in range(T - BODY, T):
                step(k, k, True, True, True)
            step(T, T, False, True, True)
            mix(T + 1, T + 1)
            pool.wait_ge(ld_att, 16 * 6)
            nc.gpsimd.tensor_tensor(qk[:, :], rmsb[:, :], qvb[:, :], ALU.mult).then_inc(qk_ready, 1)
            for m in range(4):
                pool.wait_ge(x3_dve if m % 2 else x3_act, m // 2 + 1)
                for g in (2 * m, 2 * m + 1):
                    ins = nc.gpsimd.tensor_tensor(x3b[:, g, :], x3[:, g, :], bet[:, :], ALU.add)
                ins.then_inc(x3b_ready, 1)
            pool.wait_ge(ms_ready, 1)
            nc.gpsimd.tensor_tensor(rs[:, :], ss[:, :], kon[:, K_HALF:K_HALF + 2], ALU.pow).then_inc(rs_ready, 1)
            for m in range(4):
                pool.wait_ge(var_ready, m + 1)
                nc.gpsimd.tensor_tensor(rstd[:, 2 * m:2 * m + 2], mv[:, 2 * m:2 * m + 2, 1], kon[:, K_HALF:K_HALF + 2],
                                        ALU.pow).then_inc(rstd_ready, 1)

        @block.vector
        def _(dve):
            nc.vector.memset(ones[:, :], 1.0)
            nc.vector.memset(cmax1[:, :], 1.0)
            dve.wait_ge(ld_coup, 16 * R)
            nc.vector.tensor_reduce(cmax[:, :], coup[:, :, :].rearrange("p r n -> p (r n)"), AX_X, ALU.max,
                                    apply_absolute_value=True).then_inc(cmax_ready, 1)
            dve.wait_ge(cmax_row, 1)
            nc.vector.tensor_reduce(cmax1[:, 0:1], p_gru[1][0:1, 0:P], AX_X, ALU.max).then_inc(unit_step, 1)
            dve.wait_ge(unit_step, 1)
            nc.vector.tensor_scalar(cmax1[:, 1:2], cmax1[:, 0:1], 2.0 ** -60, None, ALU.max).then_inc(unit_step, 1)
            dve.wait_ge(unit_step, 2)
            nc.vector.tensor_scalar(cmax1[:, 2:3].bitcast(I32), cmax1[:, 1:2].bitcast(I32), 0x7F800000, None,
                                    ALU.bitwise_and).then_inc(cmax_red, 1)
            dve.wait_ge(unit_psum, 1)
            nc.vector.tensor_scalar(unit[:, 0:1], p_gru[1][:, P:P + 1], 2.0 ** -14, None, ALU.mult).then_inc(unit_step, 1)
            dve.wait_ge(unit_step, 3)
            nc.vector.reciprocal(unit[:, 1:2], unit[:, 0:1]).then_inc(unit_step, 1)
            nc.vector.tensor_scalar(unit[:, 2:3], unit[:, 0:1], C, None, ALU.mult)
            nc.vector.tensor_scalar(unit[:, 3:4], unit[:, 0:1], C / 3, None, ALU.mult).then_inc(unit_ready, 1)
            dve.wait_ge(coupT_psum, 1)
            dve.wait_ge(unit_step, 4)
            src = p_gru[0][:, :]
            hi = w_hi[:, :, :, :].rearrange("p a b n -> p (a b n)")
            lo = w_lo[:, :, :, :].rearrange("p a b n -> p (a b n)")
            nc.vector.tensor_scalar(hi, src, unit[:, 1:2], None, ALU.mult).then_inc(w_hi_ready, 1)
            dve.wait_ge(w_hi_ready, 1)
            nc.vector.scalar_tensor_tensor(out=lo, in0=src, scalar=unit[:, 1:2], in1=hi, op0=ALU.mult,
                                           op1=ALU.subtract).then_inc(w_ready, 1)
            dve.wait_ge(start_ready, 1)
            nc.vector.tensor_copy(hT[:, :], condT[:, :]).then_inc(hT_ready, 1)
            nc.vector.tensor_copy(q1raw[:, :], condT[:, :]).then_inc(q_ready, 1)
            dve.wait_ge(unit_ready, 1)

            def linear(out_ap, in0, scalar, in1):
                nc.vector.scalar_tensor_tensor(out=out_ap, in0=in0, scalar=scalar, in1=in1, op0=ALU.mult,
                                               op1=ALU.add).then_inc(lin_done, 1)

            def tanh_low(t, s):
                dve.wait_ge(t_ready, t * 4 + s)
                nc.vector.tensor_tensor(t_lo[:, :], t_full[:, :], t_hi[:, :], ALU.subtract).then_inc(t_lo_ready, 1)

            def cubic(t, s):
                dve.wait_ge(sq_ready, t * 4 + s)
                nc.vector.scalar_tensor_tensor(out=g3[:, :], in0=sq[:, :], scalar=-3.0, in1=q_of[s][:, :], op0=ALU.add,
                                               op1=ALU.mult).then_inc(g3_ready, 1)

            def stage_end(t, s):
                lin = {1: lin2[:, :], 2: lin3[:, :], 3: lin4[:, 1, :], 4: linf[:, 3, :]}[s]
                dve.wait_ge(g3_ready, t * 4 + s)
                if s == 1:
                    dve.wait_ge(lin2_ready, t + 1)
                elif s == 2:
                    dve.wait_ge(lin_done, lin_count(t, "l3"))
                elif s == 3:
                    dve.wait_ge(lin_done, lin_count(t, "l4b"))
                else:
                    dve.wait_ge(lin_done, lin_count(t, "lf"))
                k3 = -C / 3 if s < 4 else -2 * C / 9
                nc.vector.scalar_tensor_tensor(out=base[:, :], in0=g3[:, :], scalar=k3, in1=lin, op0=ALU.mult,
                                               op1=ALU.add).then_inc(base_ready, 1)
                dve.wait_ge(base_ready, t * 4 + s)
                dve.wait_ge(coupled, t * 4 + s)
                u = unit[:, 2:3] if s < 4 else unit[:, 3:4]
                dst = q1raw if s == 4 else q_of[s + 1]
                nc.vector.scalar_tensor_tensor(out=dst[:, :], in0=p_l0[:, 0:W], scalar=u, in1=base[:, :], op0=ALU.mult,
                                               op1=ALU.add).then_inc(q_ready, 1)

            def clip(t, k):
                dve.wait_ge(q_ready, t * 4 + 1)
                if k == 0:
                    nc.vector.tensor_copy(q1[:, :], q1raw[:, :]).then_inc(clipped, 1)
                else:
                    nc.vector.tensor_scalar(q1[:, :], q1raw[:, :], -CLAMP, CLAMP, ALU.max, ALU.min).then_inc(clipped, 1)

            def cell_rn(u, par):
                dve.wait_ge(rz_ready, u + 1)
                nc.vector.scalar_tensor_tensor(out=rn[:, :], in0=rz[:, 0, :], scalar=1.0, in1=p_gru[par][:, 192:256],
                                               op0=ALU.add, op1=ALU.mult).then_inc(rn_ready, 1)

            def cell_pre(u, par):
                dve.wait_ge(rn_ready, u + 1)
                nc.vector.scalar_tensor_tensor(out=pre[:, :], in0=rn[:, :], scalar=0.5, in1=p_gru[par][:, 0:64],
                                               op0=ALU.mult, op1=ALU.add).then_inc(pre_ready, 1)

            def cell_un(u):
                dve.wait_ge(n_ready, u + 1)
                nc.vector.scalar_tensor_tensor(out=un[:, :], in0=zg[:, :], scalar=-1.0, in1=ng[:, :], op0=ALU.add,
                                               op1=ALU.mult).then_inc(un_ready, 1)

            def cell_h(u):
                dve.wait_ge(zh_ready, u + 1)
                dve.wait_ge(un_ready, u + 1)
                nc.vector.tensor_tensor(hB[:, :], zh[:, :], un[:, :], ALU.subtract).then_inc(hB_ready, 1)

            def cell_t(u, k):
                dve.wait_ge(hB_ready, u + 1)
                if k > 2:
                    dve.wait_ge(x2_ready, u)
                nc.vector.transpose(hT[:, :], hB[:, :]).then_inc(hT_ready, 1)

            def step(t, k, gates):
                par = k % 2
                clip(t, k)
                dve.wait_ge(clipped, t + 1)
                dve.wait_ge(p_ready, t + 1)
                linear(psum_acc[:, 0, :], pu[:, :], PU * PNC[0] / PNC[1], q1[:, :])
                tanh_low(t, 1)
                cubic(t, 1)
                dve.wait_ge(z34_ready, t + 1)
                linear(lin3[:, :], q1[:, :], L3C[1], z[:, 1, :])
                stage_end(t, 1)
                if gates:
                    cell_rn(t - 2, par)
                dve.wait_ge(lin_done, lin_count(t, "pa"))
                dve.wait_ge(q_ready, t * 4 + 2)
                linear(psum_acc[:, 1, :], psum_acc[:, 0, :], PNC[1] / PNC[2], q2[:, :])
                if gates:
                    cell_pre(t - 2, par)
                linear(lin4[:, 0, :], q1[:, :], L4C[1], z[:, 2, :])
                tanh_low(t, 2)
                cubic(t, 2)
                if gates:
                    cell_un(t - 2)
                stage_end(t, 2)
                if gates:
                    cell_h(t - 2)
                dve.wait_ge(lin_done, lin_count(t, "l4a"))
                linear(lin4[:, 1, :], q2[:, :], L4C[2], lin4[:, 0, :])
                if gates:
                    cell_t(t - 2, k)
                dve.wait_ge(zf_ready, t + 1)
                linear(linf[:, 0, :], q1[:, :], LFC[1], zf[:, :])
                tanh_low(t, 3)
                cubic(t, 3)
                dve.wait_ge(lin_done, lin_count(t, "lfa"))
                linear(linf[:, 1, :], q2[:, :], LFC[2], linf[:, 0, :])
                stage_end(t, 3)
                dve.wait_ge(lin_done, lin_count(t, "lfb"))
                linear(linf[:, 2, :], q3[:, :], LFC[3], linf[:, 1, :])
                linear(psum_acc[:, 2, :], psum_acc[:, 1, :], PNC[2] / PNC[3], q3[:, :])
                dve.wait_ge(q_ready, t * 4 + 4)
                dve.wait_ge(lin_done, lin_count(t, "lfc"))
                linear(linf[:, 3, :], q4h[:, :], 2 * LFC[4], linf[:, 2, :])
                dve.wait_ge(lin_done, lin_count(t, "pc"))
                linear(pn[:, 1, :], psum_acc[:, 2, :], PNC[3] / PU, q4h[:, :])
                tanh_low(t, 4)
                cubic(t, 4)
                stage_end(t, 4)

            for t in range(PEEL):
                step(t, t, t >= 2)
            for k in range(PEEL, T - BODY):
                step(k, k, True)
            for k in range(T - BODY, T):
                step(k, k, True)
            clip(T, T)
            for k in (T, T + 1):
                cell_rn(k - 2, k % 2)
                cell_pre(k - 2, k % 2)
                cell_un(k - 2)
                cell_h(k - 2)
                cell_t(k - 2, k)

            for m in (1, 3):
                dve.wait_ge(x3_psum, m + 1)
                nc.vector.tensor_copy(x3[:, 2 * m:2 * m + 2, :], p_x3[:, 2 * m:2 * m + 2, :]).then_inc(x3_dve, 1)
            dve.wait_ge(blk_psum, 1)
            nc.vector.tensor_copy(blk[:, :, :].rearrange("p h n -> p (h n)"), p_x[:, :]).then_inc(blk_ready, 1)
            dve.wait_ge(key_psum, 1)
            dve.wait_ge(qk_ready, 1)
            nc.vector.tensor_tensor_reduce(out=junk[:, 1, :], in0=p_gru[1][:, 0:N], in1=qk[:, :], scale=1.0, scalar=0.0,
                                           op0=ALU.mult, op1=ALU.add, accum_out=sc[:, 1:2]).then_inc(sc_ready, 1)
            dve.wait_ge(ss_ready, 1)
            nc.vector.tensor_tensor_reduce(out=junk[:, 2, :], in0=p_gru[0][:, 0:N], in1=qk[:, :], scale=1.0, scalar=0.0,
                                           op0=ALU.mult, op1=ALU.add, accum_out=sc[:, 0:1]).then_inc(sc_ready, 1)
            dve.wait_ge(ss_ready, 2)
            nc.vector.tensor_scalar(ss[:, :], ss[:, :], 1.0 / N, EPS, ALU.mult, ALU.add).then_inc(ms_ready, 1)
            dve.wait_ge(rs_ready, 1)
            dve.wait_ge(sc_ready, 2)
            nc.vector.tensor_tensor(score[:, :], sc[:, :], rs[:, :], ALU.mult).then_inc(score_ready, 1)
            dve.wait_ge(scoreT_psum, 1)
            row = p_gru[0][0:2, 0:P].rearrange("p (b n) -> p b n", n=NBLK)
            spread = [mx[:, n, :].rearrange("p (b o) -> p b o", o=1).broadcast_to([2, 16, NBLK]) for n in range(3)]
            nc.vector.tensor_reduce(mx[:, 0, :], row, AX_X, ALU.max).then_inc(soft_step, 1)
            dve.wait_ge(soft_step, 1)
            nc.vector.tensor_tensor(sm[:, :].rearrange("p (b n) -> p b n", n=NBLK), row, spread[0],
                                    ALU.subtract).then_inc(soft_step, 1)
            dve.wait_ge(exp_ready, 1)
            nc.vector.tensor_reduce(mx[:, 1, :], ex[:, :].rearrange("p (b n) -> p b n", n=NBLK), AX_X, ALU.add).then_inc(soft_step, 1)
            dve.wait_ge(soft_step, 3)
            nc.vector.reciprocal(mx[:, 2, :], mx[:, 1, :]).then_inc(soft_step, 1)
            dve.wait_ge(soft_step, 4)
            nc.vector.tensor_tensor(att[:, :].rearrange("p (b n) -> p b n", n=NBLK),
                                    ex[:, :].rearrange("p (b n) -> p b n", n=NBLK), spread[2], ALU.mult).then_inc(att_ready, 1)
            dve.wait_ge(attc_psum, 1)
            for half in range(2):
                ins = nc.vector.tensor_scalar(attb[:, half, :], kon[:, K_BD:K_BD + 16], p_gru[1][:, half:half + 1], None, ALU.mult)
            ins.then_inc(attb_ready, 1)
            dve.wait_ge(attT_psum, 1)
            nc.vector.tensor_copy(attT[:, :, :].rearrange("p c b -> p (c b)"), p_l0[:, 0:2 * B]).then_inc(attT_ready, 1)
            dve.wait_ge(prj_psum, 1)
            nc.vector.tensor_copy(prj[0:B, :], p_x[0:B, 0:N]).then_inc(prj_step, 1)
            dve.wait_ge(prj_step, 1)
            nc.vector.tensor_tensor(prt[:, :], p_x[0:B, 0:N], prj[0:B, :], ALU.subtract).then_inc(prj_step, 1)
            dve.wait_ge(prj_step, 2)
            nc.vector.tensor_copy(prm[:, :], prt[:, :]).then_inc(prj_step, 1)
            nc.vector.tensor_copy(prj[32:64, :], prt[:, :])
            dve.wait_ge(prj_step, 3)
            nc.vector.tensor_tensor(prj[64:96, :], prt[:, :], prm[:, :], ALU.subtract).then_inc(prj_ready, 1)

            def stats(m):
                dve.wait_ge(y_psum, m + 1)
                for g in (2 * m, 2 * m + 1):
                    ins = nc.vector.bn_stats(st6[:, g, :], p_x3[:, g, :])
                ins.then_inc(stat_done, 1)
                dve.wait_ge(stat_done, 2 * m + 1)
                for g in (2 * m, 2 * m + 1):
                    ins = nc.vector.bn_aggr(mv[:, g, :], st6[:, g, :])
                ins.then_inc(stat_done, 1)
                dve.wait_ge(stat_done, 2 * m + 2)
                nc.vector.tensor_scalar(mv[:, 2 * m:2 * m + 2, 1], mv[:, 2 * m:2 * m + 2, 1], EPS, None, ALU.add).then_inc(var_ready, 1)

            def norm(m):
                for g in (2 * m, 2 * m + 1):
                    nc.vector.scalar_tensor_tensor(out=nrm[:, g % 2, :], in0=p_x3[:, g, :], scalar=mv[:, g, 0:1], in1=gam[:, :],
                                                   op0=ALU.subtract, op1=ALU.mult).then_inc(nrm_ready, 1)
                dve.wait_ge(rstd_ready, m + 1)
                dve.wait_ge(x3b_ready, m + 1)
                for g in (2 * m, 2 * m + 1):
                    dve.wait_ge(nrm_ready, g + 1)
                    nc.vector.scalar_tensor_tensor(out=yout[:, g, :], in0=nrm[:, g % 2, :], scalar=rstd[:, g:g + 1],
                                                   in1=x3b[:, g, :], op0=ALU.mult, op1=ALU.add).then_inc(y_ready, 1)

            for m in range(4):
                stats(m)
                norm(m)


_INS = ["x", "cond_2048", "L0_cond_coupling", "L0_cond_bias", "L1_cond_W_ih", "L1_cond_W_hh", "L1_cond_b_ih",
        "L1_cond_b_hh", "L3_cond_rms_weight", "L3_cond_Wk", "L3_cond_Wo", "L3_cond_ln_gamma", "L3_cond_ln_beta"]


def kernel(**inputs):
    import concourse.bacc as _bacc
    from concourse.bass_utils import run_bass_kernel_spmd as _run

    nc = _bacc.Bacc("TRN2", target_bir_lowering=False, num_devices=1)
    arrays, args = {}, []
    named = [(n, np.ascontiguousarray(inputs[n])) for n in _INS]
    named += list(zip(("const_tables", "const_spread", "const_bias_rows"), constants()))
    for name, a in named:
        arrays[f"in_{name}_dram"] = a
        args.append(nc.dram_tensor(f"in_{name}_dram", a.shape, mybir.dt.from_np(a.dtype), kind="ExternalInput").ap())
    res = nc.dram_tensor("out_0_dram", (B, T, N), F32, kind="ExternalOutput").ap()
    build(nc, *args, res)
    r = _run(nc, [arrays], core_ids=[0])
    return r.results[0]["out_0_dram"]
```

```python
from contextlib import ExitStack

import numpy as np

import concourse.bass as bass
from concourse import mybir

F32 = mybir.dt.float32
BF16 = mybir.dt.bfloat16
F16 = mybir.dt.float16
I32 = mybir.dt.int32
ALU = mybir.AluOpType
ACT = mybir.ActivationFunctionType
AX_X = mybir.AxisListType.X

P = 128
B, T, N = 32, 32, 256
R = N // P
J = 4
W = R * B
TILES = B // 4
PEEL, BODY = 4, 4
NBLK = 8
EPS = 1e-6

DT, EPSN, ALPHA, BETA, CLAMP = 0.01, 0.08, 0.7, 0.8, 20.0
C = 0.5 * DT
SHIFT = ALPHA / BETA


def stage_coefficients():
    e = np.eye(5)
    p, q1, q2, q3, q4 = e
    a = EPSN * C
    p2 = p + a * (q1 - BETA * p)
    p3 = p + a * (q2 - BETA * p2)
    p4 = p + 2 * a * (q3 - BETA * p3)
    pn = p + a / 3 * ((q1 - BETA * p) + 2 * (q2 - BETA * p2) + 2 * (q3 - BETA * p3) + (q4 - BETA * p4))
    l3 = q1 - C * p2
    l4 = (q1 - 2 * C * p3) / 2
    lf = (-q1 + q2 + 2 * q3 + q4) / 3 - C / 3 * p4
    return l3, l4, lf, pn


L3C, L4C, LFC, PNC = (tuple(float(v) for v in x) for x in stage_coefficients())
PU = 2 * PNC[4]

K_ID, K_FEAT, K_IND, K_BD, K_HALF, K_END = 0, 128, 130, 162, 178, 182


def constants():
    k = np.zeros((P, K_END), np.float32)
    k[:, K_ID:K_ID + P] = np.eye(P)
    p = np.arange(P)
    for r in range(R):
        k[:, K_FEAT + r] = -(P * r + p)
    k[p, K_IND + (p // T) * NBLK + (p % T) // (T // NBLK)] = 1
    k[p, K_BD + p // NBLK] = 1
    k[:, K_HALF:K_HALF + 4] = -0.5
    bsel = np.zeros((P, P), np.float32)
    for part in range(3):
        for j in range(J):
            for s in range(2):
                bsel[32 * part + 2 * j + s, 32 * j:32 * j + 32] = 1
    return k, bsel


def build(nc, x, cond, coupling, l0_bias, w_ih, w_hh, b_ih, b_hh, rms_w, wk, wo, gamma, beta, konst, kbsel, out):
    with ExitStack() as ctx:
        def sb(name, shape, dt=F32):
            return ctx.enter_context(nc.sbuf_tensor(name, shape, dt))

        def ps(name, shape, dt=F32):
            return ctx.enter_context(nc.psum_tensor(name, shape, dt))

        def sem(name):
            return ctx.enter_context(nc.semaphore(name))

        kon = sb("kon", [P, K_END])
        bselw = sb("bselw", [P, P])
        bselb = sb("bselb", [P, P], BF16)
        coup = sb("coup", [P, R, N])
        cmax = sb("cmax", [P, 3])
        unit = sb("unit", [P, 4])
        w_hi = sb("w_hi", [P, R, R, P], F16)
        w_lo = sb("w_lo", [P, R, R, P], F16)
        condn = sb("condn", [B + 1, N])
        condT = sb("condT", [P, W])
        xn = sb("xn", [P, TILES, N])
        xT = sb("xT", [P, T, W])
        drv = sb("drv", [P, T, W])
        drv3 = sb("drv3", [P, T, W])
        lb = sb("lb", [P, R])
        dbias = sb("dbias", [P, 2, R])
        q1raw = sb("q1raw", [P, W])
        q1 = sb("q1", [P, W])
        q2 = sb("q2", [P, W])
        q3 = sb("q3", [P, W])
        q4h = sb("q4h", [P, W])
        pu = sb("pu", [P, W])
        pn = sb("pn", [P, 2, W])
        psum_acc = sb("pacc", [P, 3, W])
        t_hi = sb("t_hi", [P, W], F16)
        t_lo = sb("t_lo", [P, W], F16)
        t_full = sb("t_full", [P, W])
        sq = sb("sq", [P, W])
        g3 = sb("g3", [P, W])
        base = sb("base", [P, W])
        gp = sb("gp", [P, 3, W])
        gpf = sb("gpf", [P, W])
        z = sb("z", [P, 3, W])
        zf = sb("zf", [P, W])
        lin2 = sb("lin2", [P, W])
        lin3 = sb("lin3", [P, W])
        lin4 = sb("lin4", [P, 2, W])
        linf = sb("linf", [P, 4, W])
        wih = sb("wih", [P, R, 3, N])
        whh = sb("whh", [P, R, 3, N])
        bsrc = sb("bsrc", [P, 4, 64])
        bres = sb("bres", [8, 2, N])
        bprt = sb("bprt", [8, 2, N], BF16)
        bmov = sb("bmov", [P, N], BF16)
        x1 = sb("x1", [P, 2, W])
        hT = sb("hT", [P, W])
        hB = sb("hB", [P, W])
        rz = sb("rz", [P, 2, 64])
        zg = sb("zg", [P, 64])
        rn = sb("rn", [P, 64])
        pre = sb("pre", [P, 64])
        ng = sb("ng", [P, 64])
        un = sb("un", [P, 64])
        zh = sb("zh", [P, 64])
        x2 = sb("x2", [P, R, B, T])
        gridn = sb("gridn", [P, 64])
        gridx = sb("gridx", [P, 64])
        ixb = sb("ixb", [P, B * N])
        dist = sb("dist", [P, R, N])
        hat = sb("hat", [P, B * R * N])
        wkn = sb("wkn", [P, 2, N])
        won = sb("won", [P, 2, N])
        wkT = sb("wkT", [P, 2, N])
        woT = sb("woT", [P, 2, N])
        rmsb = sb("rmsb", [P, N])
        qvb = sb("qvb", [P, N])
        qk = sb("qk", [P, N])
        gam = sb("gam", [P, N])
        bet = sb("bet", [P, N])
        x3 = xn
        x3b = drv[:, :, :].rearrange("p t w -> p (t w)").rearrange("p (g n) -> p g n", g=TILES)
        blk = sb("blk", [P, 2, N])
        blkT = sb("blkT", [P, 2, 2, P])
        junk = sb("junk", [P, 2, 2, N])
        ss = sb("ss", [P, 2])
        ms = sb("ms", [P, 2])
        sc = sb("sc", [P, 2])
        rs = sb("rs", [P, 2])
        score = sb("score", [P, 2, 32])
        soft = sb("soft", [P, 2, 4, 32])
        mx = sb("mx", [P, 2, 3, 4])
        attc = sb("attc", [P, 2, 32])
        attw = sb("attw", [P, 2, 4 * P])
        val = sb("val", [P, 2, N])
        st6 = sb("st6", [P, TILES, 6])
        mv = sb("mv", [P, TILES, 2])
        rstd = sb("rstd", [P, TILES])
        vare = sb("vare", [P, TILES])
        nmean = sb("nmean", [P, TILES])
        nbias = sb("nbias", [P, TILES])
        nrm = xT[:, :, :].rearrange("p t w -> p (t w)").rearrange("p (g n) -> p g n", g=TILES)
        yout = drv3[:, :, :].rearrange("p t w -> p (t w)").rearrange("p (g n) -> p g n", g=TILES)

        p_l0 = ps("p_l0", [P, 512])
        p_gru = [ps(f"p_gru{i}", [P, 512]) for i in range(2)]
        p_x = ps("p_x", [P, 512])
        p_x3 = ps("p_x3", [P, 4, 2, N])

        scratch = nc.dram_tensor("grid_scratch", [B, N], F32, kind="Internal").ap()

        ident = kon[:, K_ID:K_ID + P]

        ld_coup, ld_cond, ld_kon = sem("ld_coup"), sem("ld_cond"), sem("ld_kon")
        ld_grid, ld_ih, ld_hh, ld_bias, ld_att, ld_kb = sem("ld_grid"), sem("ld_ih"), sem("ld_hh"), sem("ld_bias"), sem("ld_att"), sem("ld_kb")
        ld_x = [sem(f"ld_x{i}") for i in range(2)]
        ld_ix = sem("ld_ix")
        zeroed, grid_step, grid_ready, grid_out = sem("zeroed"), sem("grid_step"), sem("grid_ready"), sem("grid_out")
        cmax_ready, cmax_psum, unit_ready, unit_step = (
            sem("cmax_ready"), sem("cmax_psum"), sem("unit_ready"), sem("unit_step"))
        coupT_psum, w_hi_ready, w_ready, condT_psum, start_ready = (
            sem("coupT_psum"), sem("w_hi_ready"), sem("w_ready"), sem("condT_psum"), sem("start_ready"))
        xT_psum, xT_ready, dbias_ready, drv_ready = sem("xT_psum"), sem("xT_ready"), sem("dbias_ready"), sem("drv_ready")
        bias_step, bias_ready, kb_ready, qk_ready = sem("bias_step"), sem("bias_ready"), sem("kb_ready"), sem("qk_ready")
        q_ready, clipped, t_hi_ready, t_ready, t_lo_ready = (
            sem("q_ready"), sem("clipped"), sem("t_hi_ready"), sem("t_ready"), sem("t_lo_ready"))
        sq_ready, g3_ready, base_ready, coupled = sem("sq_ready"), sem("g3_ready"), sem("base_ready"), sem("coupled")
        lin_done, p_ready = sem("lin_done"), sem("p_ready")
        sp2_ready, sp34_ready, spf_ready = sem("sp2_ready"), sem("sp34_ready"), sem("spf_ready")
        z2_ready, z34_ready, zf_ready, lin2_ready = sem("z2_ready"), sem("z34_ready"), sem("zf_ready"), sem("lin2_ready")
        x1_ready, x2_ready, zh_ready = sem("x1_ready"), sem("x2_ready"), sem("zh_ready")
        gate_psum, rz_ready, zg_ready, n_ready = sem("gate_psum"), sem("rz_ready"), sem("zg_ready"), sem("n_ready")
        rn_ready, pre_ready, un_ready, hB_ready, hT_ready = (
            sem("rn_ready"), sem("pre_ready"), sem("un_ready"), sem("hB_ready"), sem("hT_ready"))
        dist_ready, hat_ready, mix_ready = sem("dist_ready"), sem("hat_ready"), sem("mix_ready")
        wT_psum, wT_ready = sem("wT_psum"), sem("wT_ready")
        x3_psum, x3_act, x3_dve, x3b_ready = sem("x3_psum"), sem("x3_act"), sem("x3_dve"), sem("x3b_ready")
        blk_psum, blk_ready, blkT_psum, blkT_ready = sem("blk_psum"), sem("blk_ready"), sem("blkT_psum"), sem("blkT_ready")
        key_psum, val_psum, val_ready, ss_ready, sc_ready, ms_ready, rs_ready, score_ready = (
            sem("key_psum"), sem("val_psum"), sem("val_ready"), sem("ss_ready"), sem("sc_ready"), sem("ms_ready"),
            sem("rs_ready"), sem("score_ready"))
        soft_step, exp_ready, attw_ready, y_psum = sem("soft_step"), sem("exp_ready"), sem("attw_ready"), sem("y_psum")
        stat_done, var_ready, rstd_ready, nbias_ready, nrm_act, nrm_pool, nrm_dve, y_pool, y_dve, stored = (
            sem("stat_done"), sem("var_ready"), sem("rstd_ready"), sem("nbias_ready"), sem("nrm_act"), sem("nrm_pool"),
            sem("nrm_dve"), sem("y_pool"), sem("y_dve"), sem("stored"))

        LIN = ["pa", "l3", "pb", "l4a", "l4b", "lfa", "lfb", "pc", "lfc", "pd", "lf"]

        def lin_count(t, name):
            return len(LIN) * t + LIN.index(name) + 1

        q_of = {1: q1, 2: q2, 3: q3, 4: q4h}

        SOFT = 7

        def add_identity(engine, queue, b):
            queue.wait_ge(hat_ready, (b + 1) * R)
            diag = hat[:, b * R * N:(b + 1) * R * N].rearrange("p (r q n) -> p (r q) n", r=R, n=P)[:, 0:R * R:R + 1, :]
            engine.tensor_tensor(diag, diag, ident.rearrange("p (o n) -> p o n", o=1).broadcast_to([P, R, P]),
                                 ALU.add).then_inc(mix_ready, 1)

        block = ctx.enter_context(nc.Block())

        @block.sync
        def _(sp):
            sp.dma_start(coup[:, :, :], coupling.rearrange("(r p) n -> p r n", r=R)).then_inc(ld_coup, 16)
            sp.dma_start(condn[0:B, :], cond).then_inc(ld_cond, 16)
            sp.dma_start(condn[B:B + 1, :], l0_bias.rearrange("(o n) -> o n", o=1)).then_inc(ld_cond, 16)
            rows = x.rearrange("(g b) t n -> (b t) g n", b=4)
            for h in range(2):
                sp.dma_start(xn[:, 4 * h:4 * h + 4, :], rows[:, 4 * h:4 * h + 4, :]).then_inc(ld_x[h], 16)
            sp.wait_ge(zeroed, 1)
            bi = b_ih.rearrange("(g r j i) -> j g r i", g=3, r=R, j=J)
            bh = b_hh.rearrange("(g r j i) -> j (g r) i", g=3, r=R, j=J)
            bd = bsrc[:, :, :].rearrange("p g (r i) -> p g r i", r=R)
            sp.dma_start(bd[0:8:2, 0, :, :], bi[:, 2, :, :]).then_inc(ld_bias, 16)
            sp.dma_start(bd[0:8:2, 1:3, :, :], bi[:, 0:2, :, :]).then_inc(ld_bias, 16)
            sp.dma_start(bd[1:8:2, 1:4, :, :].rearrange("p g r i -> p (g r) i"), bh).then_inc(ld_bias, 16)
            sp.dma_start(bselw[:, :], kbsel).then_inc(ld_kb, 16)
            rows = w_ih.rearrange("(r p) m -> p r m", r=R)
            sp.dma_start(wih[:, :, 0, :], rows[:, :, 2 * N:3 * N]).then_inc(ld_ih, 16)
            sp.dma_start(wih[:, :, 1:3, :].rearrange("p r g n -> p r (g n)"), rows[:, :, 0:2 * N]).then_inc(ld_ih, 16)
            sp.dma_start(whh[:, :, :, :].rearrange("p r g n -> p r (g n)"),
                         w_hh.rearrange("(r p) m -> p r m", r=R)).then_inc(ld_hh, 16)
            sp.wait_ge(grid_ready, 1)
            sp.dma_start(scratch.rearrange("b (q f) -> (b q) f", f=64), gridx[:, :]).then_inc(grid_out, 16)
            sp.wait_ge(grid_out, 16)
            flat = scratch.rearrange("b n -> (b n)")
            for h in range(4):
                seg = B * N // 4
                sp.dma_start(ixb[:, seg * h:seg * (h + 1)],
                             flat[seg * h:seg * (h + 1)].partition_broadcast(P)).then_inc(ld_ix, 16)
            sp.dma_start(wkn[:, :, :], wk.rearrange("(c p) h -> p c h", p=P)).then_inc(ld_att, 16)
            sp.dma_start(won[:, :, :], wo.rearrange("(c p) h -> p c h", p=P)).then_inc(ld_att, 16)
            sp.dma_start(rmsb[:, :], rms_w.partition_broadcast(P)).then_inc(ld_att, 16)
            sp.dma_start(gam[:, :], gamma.partition_broadcast(P)).then_inc(ld_att, 16)
            sp.dma_start(bet[:, :], beta.partition_broadcast(P)).then_inc(ld_att, 16)
            sp.dma_start(qvb[:, :], cond[1, :].partition_broadcast(P)).then_inc(ld_att, 16)
            for g in range(TILES):
                m, k = g // 2, g % 2
                sp.wait_ge(y_dve if m % 2 else y_pool, m // 2 * 2 + k + 1)
                sp.dma_start(out[4 * g:4 * g + 4, :, :].rearrange("b t n -> (b t) n"), yout[:, g, :]).then_inc(stored, 16)
            sp.wait_ge(stored, 16 * TILES)

        @block.scalar
        def _(act):
            act.dma_start(kon[:, :], konst).then_inc(ld_kon, 16)
            act.dma_start(gridn[:, :], cond.rearrange("b (q f) -> (b q) f", f=64)).then_inc(ld_grid, 16)

            act.wait_ge(condT_psum, 1)
            cp = p_l0[:, 0:R * (B + 1)].rearrange("p (r b) -> p r b", r=R)
            nc.scalar.copy(condT[:, :].rearrange("p (r b) -> p r b", r=R), cp[:, :, 0:B])
            nc.scalar.copy(lb[:, :].rearrange("p (r o) -> p r o", o=1), cp[:, :, B:B + 1]).then_inc(start_ready, 1)

            def scale_p(t, which):
                act.wait_ge(p_ready, t + 1)
                if which == "f":
                    nc.scalar.mul(gpf[:, :], pu[:, :], -PU * LFC[0]).then_inc(spf_ready, 1)
                elif which == 2:
                    nc.scalar.mul(gp[:, 0, :], pu[:, :], PU * C).then_inc(sp2_ready, 1)
                else:
                    nc.scalar.mul(gp[:, 1, :], pu[:, :], -PU * L3C[0])
                    nc.scalar.mul(gp[:, 2, :], pu[:, :], -PU * L4C[0]).then_inc(sp34_ready, 1)

            def hat_dist(b, r):
                nc.scalar.activation(dist[:, r, :], ixb[:, bass.ds(b * N, N)], ACT.Abs,
                                     bias=kon[:, K_FEAT + r:K_FEAT + r + 1]).then_inc(dist_ready, 1)

            def hat_weight(b, r):
                act.wait_ge(dist_ready, b * R + (r + 1))
                nc.scalar.activation(hat[:, bass.ds(b * R * N + r * N, N)], dist[:, r, :], ACT.Relu,
                                     bias=1.0, scale=-1.0).then_inc(hat_ready, 1)

            def gate_rz(u):
                act.wait_ge(gate_psum, u + 1)
                nc.scalar.activation(rz[:, :, :].rearrange("p g f -> p (g f)"), p_gru[u_parity[0]][:, 64:192],
                                     ACT.Tanh, scale=0.5).then_inc(rz_ready, 1)
                act.wait_ge(rz_ready, u + 1)
                if u + 2 < T:
                    scale_p(u + 2, "f")
                nc.scalar.activation(zg[:, :], rz[:, 1, :], ACT.Copy, bias=0.5, scale=0.5).then_inc(zg_ready, 1)

            def gate_n(u):
                act.wait_ge(pre_ready, u + 1)
                nc.scalar.activation(ng[:, :], pre[:, :], ACT.Tanh).then_inc(n_ready, 1)

            u_parity = [0]

            def step(t, k, network, gates, hats):
                u_parity[0] = k % 2
                for s in range(1, 5):
                    if network:
                        src = q1raw if s == 1 else q_of[s]
                        scale = 2.0 if s == 4 else 1.0
                        act.wait_ge(q_ready, t * 4 + s)
                        nc.scalar.activation(t_hi[:, :], src[:, :], ACT.Tanh, scale=scale).then_inc(t_hi_ready, 1)
                        nc.scalar.activation(t_full[:, :], src[:, :], ACT.Tanh, scale=scale).then_inc(t_ready, 1)
                        if s == 1:
                            act.wait_ge(clipped, t + 1)
                        nc.scalar.activation(sq[:, :], q_of[s][:, :], ACT.Square, scale=scale).then_inc(sq_ready, 1)
                    if s == 1:
                        if gates:
                            gate_rz(t - 2)
                        elif network:
                            scale_p(t, "f")
                        if hats:
                            hat_dist(t - PEEL, 0)
                    if s == 2:
                        if gates:
                            gate_n(t - 2)
                        if hats:
                            hat_weight(t - PEEL, 0)
                        if t == 0:
                            act.wait_ge(ld_kb, 16)
                            nc.scalar.copy(bselb[:, :], bselw[:, :]).then_inc(kb_ready, 1)
                    if s == 3:
                        if hats:
                            hat_dist(t - PEEL, 1)
                            hat_weight(t - PEEL, 1)
                    if s == 4:
                        if network and k != T - 1:
                            scale_p(t + 1, 2)
                            scale_p(t + 1, 34)

            for h in range(2):
                for r in range(R):
                    act.wait_ge(xT_psum, R * h + r + 1)
                    ins = nc.scalar.copy(xT[:, :, 32 * r + 16 * h:32 * r + 16 * h + 16].rearrange("p t b -> p b t"),
                                         p_x3[:, R * h + r, :, :].rearrange(
                                             "p g n -> p (g n)").rearrange("p (b t) -> p b t", t=T))
            ins.then_inc(xT_ready, 1)
            scale_p(0, 2)
            scale_p(0, 34)
            for t in range(PEEL):
                step(t, t, True, t >= 2, False)
            act.wait_ge(ld_ix, 16 * 4)
            for k in range(PEEL, T - BODY):
                step(k, k, True, True, True)
            for k in range(T - BODY, T):
                step(k, k, True, True, True)
            for b in range(T - PEEL, T):
                if b == T - PEEL:
                    step(T, T, False, True, False)
                if b == T - PEEL + 2:
                    step(T + 1, T + 1, False, True, False)
                for r in range(R):
                    hat_dist(b, r)
                    hat_weight(b, r)
                if b == T - PEEL + 1:
                    act.wait_ge(wT_psum, 1)
                    nc.scalar.copy(wkT[:, :, :].rearrange("p c n -> p (c n)"), p_x[:, :]).then_inc(wT_ready, 1)
                    act.wait_ge(wT_psum, 2)
                    nc.scalar.copy(woT[:, :, :].rearrange("p c n -> p (c n)"), p_l0[:, :]).then_inc(wT_ready, 1)

            def sampled(g):
                act.wait_ge(x3_psum, g + 1)
                nc.scalar.copy(x3[:, g, :], p_x3[:, g % 4, g // 4, :]).then_inc(x3_act, 1)

            def keys(h):
                act.wait_ge(blkT_psum, h + 1)
                nc.scalar.copy(blkT[:, h, :, :].rearrange("p c n -> p (c n)"), p_l0[:, h * N:h * N + N]).then_inc(blkT_ready, 1)

            def squares(h):
                act.wait_ge(key_psum, h + 1)
                nc.scalar.activation(junk[:, h, 0, :], p_gru[h][:, 0:N], ACT.Square, scale=N ** -0.5,
                                     accum_out=ss[:, h:h + 1]).then_inc(ss_ready, 1)
                act.wait_ge(val_psum, h + 1)
                nc.scalar.copy(val[:, h, :], p_gru[1 - h][:, N:2 * N]).then_inc(val_ready, 1)

            def exps(h):
                act.wait_ge(soft_step, SOFT * h + 3)
                nc.scalar.activation(soft[:, h, 2, :], soft[:, h, 1, :], ACT.Exp).then_inc(exp_ready, 1)

            def norms(m):
                act.wait_ge(nbias_ready, m // 2 + 1)
                for g in (2 * m, 2 * m + 1):
                    nc.scalar.activation(nrm[:, g, :], p_x3[:, g % 4, g // 4, :], ACT.Identity, bias=nbias[:, g:g + 1],
                                         scale=rstd[:, g:g + 1]).then_inc(nrm_act, 1)

            sampled(0)
            sampled(2)
            sampled(4)
            keys(0)
            squares(0)
            sampled(6)
            exps(0)
            keys(1)
            squares(1)
            norms(0)
            exps(1)
            norms(2)

        @block.tensor
        def _(pe):
            pe.wait_ge(ld_coup, 16)
            pe.wait_ge(ld_kon, 16)
            for rm in range(R):
                for rnn in range(R):
                    c0 = (rm * R + rnn) * P
                    ins = nc.tensor.transpose(p_gru[0][:, c0:c0 + P], coup[:, rnn, P * rm:P * rm + P], ident)
            ins.then_inc(coupT_psum, 1)
            pe.wait_ge(ld_cond, 32)
            for r in range(R):
                ins = nc.tensor.transpose(p_l0[:, (B + 1) * r:(B + 1) * (r + 1)], condn[:, P * r:P * r + P], kon[0:B + 1, K_ID:K_ID + B + 1])
            ins.then_inc(condT_psum, 1)
            pe.wait_ge(cmax_ready, 1)
            nc.tensor.matmul(p_gru[1][:, 0:P], cmax[:, 0:1].broadcast_to([P, P]), ident, start=True, stop=True).then_inc(cmax_psum, 1)
            for h in range(2):
                pe.wait_ge(ld_x[h], 16)
                for r in range(R):
                    for g in range(4):
                        ins = nc.tensor.transpose(p_x3[:, R * h + r, g // 2, P * (g % 2):P * (g % 2) + P],
                                                  xn[:, 4 * h + g, P * r:P * r + P], ident)
                    ins.then_inc(xT_psum, 1)
            pe.wait_ge(w_ready, 1)

            def couple(w, tt, first, last):
                for rnn in range(R):
                    for rm in range(R):
                        ins = nc.tensor.matmul(p_l0[:, 32 * rnn:32 * rnn + 32], w[:, rm, rnn, :], tt[:, 32 * rm:32 * rm + 32],
                                               start=first and rnn == 0 and rm == 0, stop=last and rm == R - 1,
                                               skip_group_check=True)
                return ins

            def gate_bias(par):
                nc.tensor.matmul(p_gru[par][:, 0:N], bselb[:, :], bmov[:, :], start=True, stop=False, skip_group_check=True)

            def gate_x(par, r):
                for j in range(J):
                    nc.tensor.matmul(p_gru[par][32 * j:32 * j + 32, 0:192], x1[:, par, 32 * r:32 * r + 32],
                                     wih[:, r, :, :].rearrange("p g (q i) -> p g q i", q=R)[:, :, :, 32 * j:32 * j + 32], start=False, stop=False, skip_group_check=True)

            def gate_h(par, r):
                for j in range(J):
                    ins = nc.tensor.matmul(p_gru[par][32 * j:32 * j + 32, 64:256], hT[:, 32 * r:32 * r + 32],
                                           whh[:, r, :, :].rearrange("p g (q i) -> p g q i", q=R)[:, :, :, 32 * j:32 * j + 32], start=False, stop=(r == R - 1),
                                           skip_group_check=True)
                if r == R - 1:
                    ins.then_inc(gate_psum, 1)

            def step(t, k, network, products):
                par = (k - 1) % 2
                for s in range(1, 5):
                    if network:
                        pe.wait_ge(t_hi_ready, t * 4 + s)
                        couple(w_hi, t_hi, True, False)
                        couple(w_lo, t_hi, False, False)
                    if network:
                        pe.wait_ge(t_lo_ready, t * 4 + s)
                        couple(w_hi, t_lo, False, True).then_inc(coupled, 1)
                    if s == 1 and products:
                        if k == 1:
                            pe.wait_ge(bias_ready, 1)
                            pe.wait_ge(kb_ready, 1)
                        gate_bias(par)
                    if products:
                        if s == 1:
                            if k == 1:
                                pe.wait_ge(ld_ih, 16 * 2)
                            pe.wait_ge(x1_ready, t)
                            gate_x(par, 0)
                        if s == 2:
                            gate_x(par, 1)
                        if s == 3:
                            if k == 1:
                                pe.wait_ge(ld_hh, 16)
                            pe.wait_ge(hT_ready, t)
                            gate_h(par, 0)
                        if s == 4:
                            gate_h(par, 1)

            for t in range(PEEL):
                step(t, t, True, t >= 1)
            for k in range(PEEL, T - BODY):
                step(k, k, True, True)
            for k in range(T - BODY, T):
                step(k, k, True, True)
            step(T, T, False, True)

            pe.wait_ge(ld_att, 16 * 6)
            for n, (src, dst) in enumerate(((wkn, p_x), (won, p_l0))):
                if n == 1:
                    pe.wait_ge(q_ready, 4 * T + 1)
                for ch in range(2):
                    for ck in range(2):
                        c0 = ch * N + ck * P
                        ins = nc.tensor.transpose(dst[:, c0:c0 + P], src[:, ck, P * ch:P * ch + P], ident)
                ins.then_inc(wT_psum, 1)

            def sample(g):
                pe.wait_ge(mix_ready, 4 * g + 4)
                if g >= 4:
                    pe.wait_ge(x3_dve if g % 2 else x3_act, (g - 4) // 2 + 1)
                for r in range(R):
                    for j in range(J):
                        b = 4 * g + j
                        ins = nc.tensor.matmul(p_x3[32 * j:32 * j + 32, g % 4, g // 4, :], x2[:, r, b, :],
                                               hat[:, (b * R + r) * N:(b * R + r + 1) * N],
                                               start=(r == 0 and g < 4), stop=(r == R - 1), skip_group_check=True)
                ins.then_inc(x3_psum, 1)

            def block_sums(h):
                pe.wait_ge(wT_ready, 2)
                if h == 1:
                    pe.wait_ge(blk_ready, 1)
                for g in range(4 * h, 4 * h + 4):
                    pe.wait_ge(x3_dve if g % 2 else x3_act, g // 2 + 1)
                    j = g % 4
                    ins = nc.tensor.matmul(p_x[32 * j:32 * j + 32, 0:N], kon[:, K_IND:K_IND + 32],
                                           x3[:, g, :], start=True, stop=True, skip_group_check=True)
                ins.then_inc(blk_psum, 1)

            def turn(h):
                pe.wait_ge(blk_ready, h + 1)
                for c in range(2):
                    c0 = (h * 2 + c) * P
                    ins = nc.tensor.transpose(p_l0[:, c0:c0 + P], blk[:, h, P * c:P * c + P], ident)
                ins.then_inc(blkT_psum, 1)

            def keys(h):
                pe.wait_ge(blkT_ready, h + 1)
                if h == 1:
                    pe.wait_ge(val_ready, 1)
                for c in range(2):
                    ins = nc.tensor.matmul(p_gru[h][:, 0:N], blkT[:, h, c, :], wkT[:, c, :], start=(c == 0), stop=(c == 1),
                                           skip_group_check=True)
                ins.then_inc(key_psum, 1)
                if h == 1:
                    pe.wait_ge(sc_ready, 1)
                for c in range(2):
                    ins = nc.tensor.matmul(p_gru[1 - h][:, N:2 * N], blkT[:, h, c, :], woT[:, c, :], start=(c == 0), stop=(c == 1),
                                           skip_group_check=True)
                ins.then_inc(val_psum, 1)

            def attend(h):
                pe.wait_ge(attw_ready, h + 1)
                pe.wait_ge(val_ready, h + 1)
                for g in range(4):
                    if h == 1:
                        pe.wait_ge(nrm_act if g < 2 else nrm_dve, g % 2 + 1)
                    nc.tensor.matmul(p_x3[:, g, h, :], attw[:, h, P * g:P * g + P], val[:, h, :], start=False, stop=True,
                                     skip_group_check=True).then_inc(y_psum, 1)

            pe.wait_ge(x2_ready, T)
            for g in range(5):
                sample(g)
            block_sums(0)
            sample(5)
            turn(0)
            sample(6)
            keys(0)
            sample(7)
            block_sums(1)
            turn(1)
            keys(1)
            attend(0)
            attend(1)

        @block.gpsimd
        def _(pool):
            nc.gpsimd.memset(bsrc[:, :, :], 0.0).then_inc(zeroed, 1)
            nc.gpsimd.memset(bmov[:, :], 0.0).then_inc(zeroed, 1)
            nc.gpsimd.memset(score[:, :, :], 0.0).then_inc(zeroed, 1)
            pool.wait_ge(ld_grid, 16)
            nc.gpsimd.tensor_scalar(gridn[:, :], gridn[:, :], 1.0, 0.5 * (N - 1), ALU.add, ALU.mult).then_inc(grid_step, 1)
            pool.wait_ge(grid_step, 1)
            nc.gpsimd.tensor_scalar(gridx[:, :], gridn[:, :], 0.0, float(N - 1), ALU.max, ALU.min).then_inc(grid_ready, 1)
            pool.wait_ge(start_ready, 1)
            nc.gpsimd.tensor_scalar(pu[:, :], condT[:, :], -SHIFT, 1.0 / PU, ALU.add, ALU.mult).then_inc(p_ready, 1)
            for n, c in enumerate((C, C / 3)):
                ins = nc.gpsimd.tensor_scalar(dbias[:, n, :], lb[:, :], -SHIFT, c, ALU.add, ALU.mult)
            ins.then_inc(dbias_ready, 1)
            pool.wait_ge(dbias_ready, 1)
            pool.wait_ge(xT_ready, 1)

            def drive(first, last):
                for n, (c, dst) in enumerate(((C, drv), (C / 3, drv3))):
                    for r in range(R):
                        ins = nc.gpsimd.tensor_scalar(dst[:, first:last, 32 * r:32 * r + 32],
                                                      xT[:, first:last, 32 * r:32 * r + 32],
                                                      c, dbias[:, n, r:r + 1], ALU.mult, ALU.add)
                ins.then_inc(drv_ready, 1)

            def z2(t):
                pool.wait_ge(sp2_ready, t + 1)
                nc.gpsimd.tensor_tensor(z[:, 0:1, :], drv[:, bass.ds(t, 1), :], gp[:, 0:1, :], ALU.subtract).then_inc(z2_ready, 1)

            def step(t, network, inputs, gates, hats):
                pool.wait_ge(clipped, t + 1)
                if network:
                    pool.wait_ge(z2_ready, t + 1)
                    nc.gpsimd.tensor_tensor(lin2[:, :], z[:, 0, :], q1[:, :], ALU.add).then_inc(lin2_ready, 1)
                if inputs:
                    if not network:
                        pool.wait_ge(x2_ready, t - 2)
                    nc.gpsimd.tensor_tensor(x1[:, (t - 1) % 2, :], xT[:, t - 1, :], q1[:, :], ALU.add).then_inc(x1_ready, 1)
                if network:
                    pool.wait_ge(sp34_ready, t + 1)
                    for n in (1, 2):
                        ins = nc.gpsimd.tensor_tensor(z[:, n, :], drv[:, t, :], gp[:, n, :], ALU.subtract)
                    ins.then_inc(z34_ready, 1)
                    pool.wait_ge(spf_ready, t + 1)
                    nc.gpsimd.tensor_tensor(zf[:, :], drv3[:, t, :], gpf[:, :], ALU.subtract).then_inc(zf_ready, 1)
                if t == 0:
                    drive(1, T)
                    pool.wait_ge(drv_ready, 2)
                if gates:
                    keep(t)
                if hats:
                    add_identity(nc.gpsimd, pool, t - PEEL - 1)
                if gates:
                    mix(t, t)
                if network:
                    pool.wait_ge(lin_done, lin_count(t, "pd"))
                    nc.gpsimd.tensor_scalar(pu[:, :], pn[:, 1, :], (-CLAMP - SHIFT) / PU, (CLAMP - SHIFT) / PU,
                                            ALU.max, ALU.min).then_inc(p_ready, 1)
                    if t != T - 1:
                        z2(t + 1)

            def keep(t):
                pool.wait_ge(zg_ready, t - 1)
                pool.wait_ge(hB_ready, t - 1)
                nc.gpsimd.tensor_tensor(zh[:, :], zg[:, :], hB[:, :], ALU.mult).then_inc(zh_ready, 1)

            def mix(t, k):
                pool.wait_ge(hT_ready, t)
                nc.gpsimd.tensor_tensor(x2[:, :, :, bass.ds(t - 2, 1)],
                                        x1[:, k % 2, :].rearrange("p (r b o) -> p r b o", r=R, o=1),
                                        hT[:, :].rearrange("p (r b o) -> p r b o", r=R, o=1), ALU.add).then_inc(x2_ready, 1)

            drive(0, 1)
            pool.wait_ge(drv_ready, 1)
            z2(0)
            for t in range(T + 1):
                step(t, t < T, t >= 1, t >= 2, t > PEEL)
            keep(T + 1)
            mix(T + 1, T + 1)
            pool.wait_ge(ld_att, 16 * 6)
            nc.gpsimd.tensor_tensor(qk[:, :], rmsb[:, :], qvb[:, :], ALU.mult).then_inc(qk_ready, 1)

            def shifted(g):
                pool.wait_ge(x3_dve if g % 2 else x3_act, g // 2 + 1)
                nc.gpsimd.tensor_tensor(x3b[:, g, :], x3[:, g, :], bet[:, :], ALU.add).then_inc(x3b_ready, 1)

            def key_rms(h):
                pool.wait_ge(ms_ready, h + 1)
                nc.gpsimd.tensor_tensor(rs[:, h:h + 1], ms[:, h:h + 1], kon[:, K_HALF:K_HALF + 1], ALU.pow).then_inc(rs_ready, 1)

            def deviation(m):
                two = slice(2 * m, 2 * m + 2)
                pool.wait_ge(var_ready, m + 1)
                nc.gpsimd.tensor_tensor(rstd[:, two], vare[:, two], kon[:, K_HALF:K_HALF + 2], ALU.pow).then_inc(rstd_ready, 1)
                if m % 2 == 0:
                    pool.wait_ge(rstd_ready, m + 1)
                    nc.gpsimd.tensor_tensor(nbias[:, two], nmean[:, two], rstd[:, two], ALU.mult).then_inc(nbias_ready, 1)

            def affine(m):
                for g in (2 * m, 2 * m + 1):
                    pool.wait_ge(nrm_act, m + (g % 2) + 1)
                    nc.gpsimd.tensor_tensor(nrm[:, g, :], nrm[:, g, :], gam[:, :], ALU.mult).then_inc(nrm_pool, 1)
                for g in (2 * m, 2 * m + 1):
                    pool.wait_ge(nrm_pool, m + (g % 2) + 1)
                    nc.gpsimd.tensor_tensor(yout[:, g, :], nrm[:, g, :], x3b[:, g, :], ALU.add).then_inc(y_pool, 1)

            for g in range(4):
                shifted(g)
            key_rms(0)
            for g in range(4, 8):
                shifted(g)
            key_rms(1)
            deviation(0)
            deviation(1)
            affine(0)
            deviation(2)
            deviation(3)
            affine(2)

        @block.vector
        def _(dve):
            dve.wait_ge(ld_coup, 16)
            nc.vector.tensor_reduce(cmax[:, 0:1], coup[:, :, :].rearrange("p r n -> p (r n)"), AX_X, ALU.max,
                                    apply_absolute_value=True).then_inc(cmax_ready, 1)
            dve.wait_ge(cmax_psum, 1)
            nc.vector.tensor_reduce(cmax[:, 1:2], p_gru[1][:, 0:P], AX_X, ALU.max).then_inc(unit_step, 1)
            dve.wait_ge(unit_step, 1)
            nc.vector.tensor_scalar(cmax[:, 2:3], cmax[:, 1:2], 2.0 ** -60, 2.0 ** -14, ALU.max, ALU.mult).then_inc(unit_step, 1)
            dve.wait_ge(unit_step, 2)
            nc.vector.tensor_scalar(unit[:, 0:1].bitcast(I32), cmax[:, 2:3].bitcast(I32), 0x7F800000, None,
                                    ALU.bitwise_and).then_inc(unit_step, 1)
            dve.wait_ge(unit_step, 3)
            nc.vector.reciprocal(unit[:, 1:2], unit[:, 0:1]).then_inc(unit_step, 1)
            nc.vector.tensor_scalar(unit[:, 2:3], unit[:, 0:1], C, None, ALU.mult)
            nc.vector.tensor_scalar(unit[:, 3:4], unit[:, 0:1], C / 3, None, ALU.mult).then_inc(unit_ready, 1)
            dve.wait_ge(coupT_psum, 1)
            dve.wait_ge(unit_step, 4)
            src = p_gru[0][:, :]
            hi = w_hi[:, :, :, :].rearrange("p a b n -> p (a b n)")
            lo = w_lo[:, :, :, :].rearrange("p a b n -> p (a b n)")
            nc.vector.tensor_scalar(hi, src, unit[:, 1:2], None, ALU.mult).then_inc(w_hi_ready, 1)
            dve.wait_ge(w_hi_ready, 1)
            nc.vector.scalar_tensor_tensor(out=lo, in0=src, scalar=unit[:, 1:2], in1=hi, op0=ALU.mult,
                                           op1=ALU.subtract).then_inc(w_ready, 1)
            dve.wait_ge(start_ready, 1)
            nc.vector.tensor_copy(q1raw[:, :], condT[:, :]).then_inc(q_ready, 1)
            nc.vector.tensor_copy(hT[:, :], condT[:, :]).then_inc(hT_ready, 1)
            nc.vector.transpose(hB[:, :], condT[:, :]).then_inc(hB_ready, 1)
            dve.wait_ge(unit_ready, 1)

            def bias_part(s):
                rows = bsrc[0:8, :, :].rearrange("p g f -> p (g f)")
                if s == 1:
                    dve.wait_ge(zeroed, 3)
                    dve.wait_ge(ld_bias, 48)
                    nc.vector.tensor_copy(bmov[0:8, :], rows).then_inc(bias_step, 1)
                elif s == 2:
                    dve.wait_ge(bias_step, 1)
                    nc.vector.tensor_tensor(bres[:, 0, :], rows, bmov[0:8, :], ALU.subtract).then_inc(bias_step, 1)
                elif s == 3:
                    dve.wait_ge(bias_step, 2)
                    nc.vector.tensor_copy(bprt[:, 0, :], bres[:, 0, :])
                    nc.vector.tensor_copy(bmov[32:40, :], bres[:, 0, :]).then_inc(bias_step, 1)
                else:
                    dve.wait_ge(bias_step, 3)
                    nc.vector.tensor_tensor(bmov[64:72, :], bres[:, 0, :], bprt[:, 0, :], ALU.subtract).then_inc(bias_ready, 1)

            def linear(out_ap, in0, scalar, in1):
                nc.vector.scalar_tensor_tensor(out=out_ap, in0=in0, scalar=scalar, in1=in1, op0=ALU.mult,
                                               op1=ALU.add).then_inc(lin_done, 1)

            def tanh_low(t, s):
                dve.wait_ge(t_ready, t * 4 + s)
                nc.vector.tensor_tensor(t_lo[:, :], t_full[:, :], t_hi[:, :], ALU.subtract).then_inc(t_lo_ready, 1)

            def cubic(t, s):
                dve.wait_ge(sq_ready, t * 4 + s)
                nc.vector.scalar_tensor_tensor(out=g3[:, :], in0=sq[:, :], scalar=-3.0, in1=q_of[s][:, :], op0=ALU.add,
                                               op1=ALU.mult).then_inc(g3_ready, 1)

            def base_sum(t, s):
                lin = {1: lin2[:, :], 2: lin3[:, :], 3: lin4[:, 1, :], 4: linf[:, 3, :]}[s]
                dve.wait_ge(g3_ready, t * 4 + s)
                if s == 1:
                    dve.wait_ge(lin2_ready, t + 1)
                elif s == 2:
                    dve.wait_ge(lin_done, lin_count(t, "l3"))
                elif s == 3:
                    dve.wait_ge(lin_done, lin_count(t, "l4b"))
                else:
                    dve.wait_ge(lin_done, lin_count(t, "lf"))
                k3 = -C / 3 if s < 4 else -2 * C / 9
                nc.vector.scalar_tensor_tensor(out=base[:, :], in0=g3[:, :], scalar=k3, in1=lin, op0=ALU.mult,
                                               op1=ALU.add).then_inc(base_ready, 1)

            def next_q(t, s):
                dve.wait_ge(base_ready, t * 4 + s)
                dve.wait_ge(coupled, t * 4 + s)
                u = unit[:, 2:3] if s < 4 else unit[:, 3:4]
                dst = q1raw if s == 4 else q_of[s + 1]
                nc.vector.scalar_tensor_tensor(out=dst[:, :], in0=p_l0[:, 0:W], scalar=u, in1=base[:, :], op0=ALU.mult,
                                               op1=ALU.add).then_inc(q_ready, 1)

            def clip(t, k):
                dve.wait_ge(q_ready, t * 4 + 1)
                if k == 0:
                    nc.vector.tensor_copy(q1[:, :], q1raw[:, :]).then_inc(clipped, 1)
                else:
                    nc.vector.tensor_scalar(q1[:, :], q1raw[:, :], -CLAMP, CLAMP, ALU.max, ALU.min).then_inc(clipped, 1)

            def cell_rn(u, par):
                dve.wait_ge(rz_ready, u + 1)
                nc.vector.scalar_tensor_tensor(out=rn[:, :], in0=rz[:, 0, :], scalar=1.0, in1=p_gru[par][:, 192:256],
                                               op0=ALU.add, op1=ALU.mult).then_inc(rn_ready, 1)

            def cell_pre(u, par):
                dve.wait_ge(rn_ready, u + 1)
                nc.vector.scalar_tensor_tensor(out=pre[:, :], in0=rn[:, :], scalar=0.5, in1=p_gru[par][:, 0:64],
                                               op0=ALU.mult, op1=ALU.add).then_inc(pre_ready, 1)

            def cell_un(u):
                dve.wait_ge(n_ready, u + 1)
                nc.vector.scalar_tensor_tensor(out=un[:, :], in0=zg[:, :], scalar=-1.0, in1=ng[:, :], op0=ALU.add,
                                               op1=ALU.mult).then_inc(un_ready, 1)

            def cell_h(u):
                dve.wait_ge(zh_ready, u + 1)
                dve.wait_ge(un_ready, u + 1)
                nc.vector.tensor_tensor(hB[:, :], zh[:, :], un[:, :], ALU.subtract).then_inc(hB_ready, 1)

            def cell_t(u, k):
                dve.wait_ge(hB_ready, u + 2)
                if k > 2:
                    dve.wait_ge(x2_ready, u)
                nc.vector.transpose(hT[:, :], hB[:, :]).then_inc(hT_ready, 1)

            def step(t, gates):
                par = t % 2
                clip(t, t)
                dve.wait_ge(clipped, t + 1)
                dve.wait_ge(p_ready, t + 1)
                linear(psum_acc[:, 0, :], pu[:, :], PU * PNC[0] / PNC[1], q1[:, :])
                tanh_low(t, 1)
                cubic(t, 1)
                base_sum(t, 1)
                if gates:
                    cell_rn(t - 2, par)
                if t == 0:
                    bias_part(1)
                next_q(t, 1)
                if gates:
                    cell_pre(t - 2, par)
                dve.wait_ge(z34_ready, t + 1)
                linear(lin3[:, :], q1[:, :], L3C[1], z[:, 1, :])
                dve.wait_ge(lin_done, lin_count(t, "pa"))
                dve.wait_ge(q_ready, t * 4 + 2)
                linear(psum_acc[:, 1, :], psum_acc[:, 0, :], PNC[1] / PNC[2], q2[:, :])
                linear(lin4[:, 0, :], q1[:, :], L4C[1], z[:, 2, :])
                tanh_low(t, 2)
                cubic(t, 2)
                base_sum(t, 2)
                if gates:
                    cell_un(t - 2)
                if t == 0:
                    bias_part(2)
                next_q(t, 2)
                if gates:
                    cell_h(t - 2)
                dve.wait_ge(lin_done, lin_count(t, "l4a"))
                linear(lin4[:, 1, :], q2[:, :], L4C[2], lin4[:, 0, :])
                if gates:
                    cell_t(t - 2, t)
                dve.wait_ge(zf_ready, t + 1)
                linear(linf[:, 0, :], q1[:, :], LFC[1], zf[:, :])
                tanh_low(t, 3)
                cubic(t, 3)
                dve.wait_ge(lin_done, lin_count(t, "lfa"))
                linear(linf[:, 1, :], q2[:, :], LFC[2], linf[:, 0, :])
                base_sum(t, 3)
                dve.wait_ge(lin_done, lin_count(t, "pb"))
                linear(psum_acc[:, 2, :], psum_acc[:, 1, :], PNC[2] / PNC[3], q3[:, :])
                if t == 0:
                    bias_part(3)
                next_q(t, 3)
                dve.wait_ge(lin_done, lin_count(t, "lfb"))
                linear(linf[:, 2, :], q3[:, :], LFC[3], linf[:, 1, :])
                dve.wait_ge(q_ready, t * 4 + 4)
                dve.wait_ge(lin_done, lin_count(t, "pc"))
                linear(pn[:, 1, :], psum_acc[:, 2, :], PNC[3] / PU, q4h[:, :])
                dve.wait_ge(lin_done, lin_count(t, "lfc"))
                linear(linf[:, 3, :], q4h[:, :], 2 * LFC[4], linf[:, 2, :])
                tanh_low(t, 4)
                cubic(t, 4)
                base_sum(t, 4)
                if t == 0:
                    bias_part(4)
                next_q(t, 4)

            for t in range(T):
                step(t, t >= 2)
            clip(T, T)
            for k in (T, T + 1):
                cell_rn(k - 2, k % 2)
                cell_pre(k - 2, k % 2)
                cell_un(k - 2)
                cell_h(k - 2)
                cell_t(k - 2, k)
            for b in range(T - PEEL, T):
                add_identity(nc.vector, dve, b)

            def sampled(g):
                dve.wait_ge(x3_psum, g + 1)
                nc.vector.tensor_copy(x3[:, g, :], p_x3[:, g % 4, g // 4, :]).then_inc(x3_dve, 1)

            def block_sums(h):
                dve.wait_ge(blk_psum, h + 1)
                nc.vector.tensor_copy(blk[:, h, :], p_x[:, 0:N]).then_inc(blk_ready, 1)

            def scores(h):
                dve.wait_ge(ss_ready, h + 1)
                nc.vector.tensor_scalar(ms[:, h:h + 1], ss[:, h:h + 1], EPS, None, ALU.add).then_inc(ms_ready, 1)
                dve.wait_ge(qk_ready, 1)
                nc.vector.tensor_tensor_reduce(out=junk[:, h, 1, :], in0=p_gru[h][:, 0:N], in1=qk[:, :], scale=1.0, scalar=0.0,
                                               op0=ALU.mult, op1=ALU.add, accum_out=sc[:, h:h + 1]).then_inc(sc_ready, 1)
                dve.wait_ge(zeroed, 3)
                dve.wait_ge(sc_ready, h + 1)
                dve.wait_ge(rs_ready, h + 1)
                nc.vector.tensor_tensor(score[:, h, 0:1], sc[:, h:h + 1], rs[:, h:h + 1], ALU.mult).then_inc(score_ready, 1)

            def four(ap):
                return ap.rearrange("p (b n) -> p b n", n=NBLK)

            def spread(ap):
                return ap.rearrange("p (b o) -> p b o", o=1).broadcast_to([P, 4, NBLK])

            def softmax_max(h):
                base_step = SOFT * h
                dve.wait_ge(score_ready, h + 1)
                nc.vector.transpose(soft[:, h, 0, :], score[:, h, :]).then_inc(soft_step, 1)
                dve.wait_ge(soft_step, base_step + 1)
                nc.vector.tensor_reduce(mx[:, h, 0, :], four(soft[:, h, 0, :]), AX_X, ALU.max).then_inc(soft_step, 1)
                dve.wait_ge(soft_step, base_step + 2)
                nc.vector.tensor_tensor(four(soft[:, h, 1, :]), four(soft[:, h, 0, :]), spread(mx[:, h, 0, :]),
                                        ALU.subtract).then_inc(soft_step, 1)

            def softmax_sum(h):
                base_step = SOFT * h
                dve.wait_ge(exp_ready, h + 1)
                nc.vector.tensor_reduce(mx[:, h, 1, :], four(soft[:, h, 2, :]), AX_X, ALU.add).then_inc(soft_step, 1)
                dve.wait_ge(soft_step, base_step + 4)
                nc.vector.reciprocal(mx[:, h, 2, :], mx[:, h, 1, :]).then_inc(soft_step, 1)
                dve.wait_ge(soft_step, base_step + 5)
                nc.vector.tensor_tensor(four(soft[:, h, 3, :]), four(soft[:, h, 2, :]), spread(mx[:, h, 2, :]),
                                        ALU.mult).then_inc(soft_step, 1)
                dve.wait_ge(soft_step, base_step + 6)
                nc.vector.transpose(attc[:, h, :], soft[:, h, 3, :]).then_inc(soft_step, 1)
                dve.wait_ge(soft_step, base_step + 7)
                member = kon[:, K_BD:K_BD + 16].rearrange("p (b o) -> p b o", o=1).broadcast_to([P, 16, T])
                nc.vector.tensor_scalar(attw[:, h, :].rearrange("p (b t) -> p b t", t=T), member, attc[:, h, 0:1], None,
                                        ALU.mult).then_inc(attw_ready, 1)

            def stats(m):
                two = slice(2 * m, 2 * m + 2)
                for g in (2 * m, 2 * m + 1):
                    dve.wait_ge(y_psum, g + 1)
                    ins = nc.vector.bn_stats(st6[:, g, :], p_x3[:, g % 4, g // 4, :])
                ins.then_inc(stat_done, 1)
                dve.wait_ge(stat_done, 2 * m + 1)
                for g in (2 * m, 2 * m + 1):
                    ins = nc.vector.bn_aggr(mv[:, g, :], st6[:, g, :])
                ins.then_inc(stat_done, 1)
                dve.wait_ge(stat_done, 2 * m + 2)
                nc.vector.tensor_scalar(nmean[:, two], mv[:, two, 0], -1.0, None, ALU.mult)
                nc.vector.tensor_scalar(vare[:, two], mv[:, two, 1], EPS, None, ALU.add).then_inc(var_ready, 1)

            def centre(m):
                for g in (2 * m, 2 * m + 1):
                    nc.vector.scalar_tensor_tensor(out=nrm[:, g, :], in0=p_x3[:, g % 4, g // 4, :], scalar=mv[:, g, 0:1], in1=gam[:, :],
                                                   op0=ALU.subtract, op1=ALU.mult).then_inc(nrm_dve, 1)

            def finish(m):
                dve.wait_ge(rstd_ready, m + 1)
                for g in (2 * m, 2 * m + 1):
                    dve.wait_ge(x3b_ready, g + 1)
                    dve.wait_ge(nrm_dve, m // 2 * 2 + g % 2 + 1)
                    nc.vector.scalar_tensor_tensor(out=yout[:, g, :], in0=nrm[:, g, :], scalar=rstd[:, g:g + 1],
                                                   in1=x3b[:, g, :], op0=ALU.mult, op1=ALU.add).then_inc(y_dve, 1)

            sampled(1)
            sampled(3)
            block_sums(0)
            sampled(5)
            scores(0)
            softmax_max(0)
            sampled(7)
            softmax_sum(0)
            block_sums(1)
            scores(1)
            softmax_max(1)
            stats(0)
            softmax_sum(1)
            stats(1)
            centre(1)
            stats(2)
            finish(1)
            stats(3)
            centre(3)
            finish(3)


_INS = ["x", "cond_2048", "L0_cond_coupling", "L0_cond_bias", "L1_cond_W_ih", "L1_cond_W_hh", "L1_cond_b_ih",
        "L1_cond_b_hh", "L3_cond_rms_weight", "L3_cond_Wk", "L3_cond_Wo", "L3_cond_ln_gamma", "L3_cond_ln_beta"]


def kernel(**inputs):
    import concourse.bacc as _bacc
    from concourse.bass_utils import run_bass_kernel_spmd as _run

    nc = _bacc.Bacc("TRN2", target_bir_lowering=False, num_devices=1)
    arrays, args = {}, []
    named = [(n, np.ascontiguousarray(inputs[n])) for n in _INS]
    named += list(zip(("const_tables", "const_bias_rows"), constants()))
    for name, a in named:
        arrays[f"in_{name}_dram"] = a
        args.append(nc.dram_tensor(f"in_{name}_dram", a.shape, mybir.dt.from_np(a.dtype), kind="ExternalInput").ap())
    res = nc.dram_tensor("out_0_dram", (B, T, N), F32, kind="ExternalOutput").ap()
    build(nc, *args, res)
    r = _run(nc, [arrays], core_ids=[0])
    return r.results[0]["out_0_dram"]
```

```python
from contextlib import ExitStack

import numpy as np

import concourse.bass as bass
from concourse import mybir

F32 = mybir.dt.float32
BF16 = mybir.dt.bfloat16
F16 = mybir.dt.float16
I32 = mybir.dt.int32
ALU = mybir.AluOpType
ACT = mybir.ActivationFunctionType
AX_X = mybir.AxisListType.X

P = 128
B, T, N = 32, 32, 256
R = N // P
J = 4
W = R * B
TILES = B // 4
FIRST = 3
HALFWAY = 14
PEEL = 3
NBLK = 8
EPS = 1e-6

DT, EPSN, ALPHA, BETA, CLAMP = 0.01, 0.08, 0.7, 0.8, 20.0
C = 0.5 * DT
SHIFT = ALPHA / BETA


def stage_coefficients():
    e = np.eye(5)
    p, q1, q2, q3, q4 = e
    a = EPSN * C
    p2 = p + a * (q1 - BETA * p)
    p3 = p + a * (q2 - BETA * p2)
    p4 = p + 2 * a * (q3 - BETA * p3)
    pn = p + a / 3 * ((q1 - BETA * p) + 2 * (q2 - BETA * p2) + 2 * (q3 - BETA * p3) + (q4 - BETA * p4))
    l3 = q1 - C * p2
    l4 = (q1 - 2 * C * p3) / 2
    lf = (-q1 + q2 + 2 * q3 + q4) / 3 - C / 3 * p4
    return l3, l4, lf, pn


L3C, L4C, LFC, PNC = (tuple(float(v) for v in x) for x in stage_coefficients())
PU = 2 * PNC[4]

K_ID, K_FEAT, K_IND, K_BD, K_HALF, K_END = 0, 128, 130, 162, 178, 182


def constants():
    k = np.zeros((P, K_END), np.float32)
    k[:, K_ID:K_ID + P] = np.eye(P)
    p = np.arange(P)
    for r in range(R):
        k[:, K_FEAT + r] = -(P * r + p)
    k[p, K_IND + (p // T) * NBLK + (p % T) // (T // NBLK)] = 1
    k[p, K_BD + p // NBLK] = 1
    k[:, K_HALF:K_HALF + 4] = -0.5
    bsel = np.zeros((P, P), np.float32)
    for part in range(3):
        for j in range(J):
            for s in range(2):
                bsel[32 * part + 2 * j + s, 32 * j:32 * j + 32] = 1
    return k, bsel


def build(nc, x, cond, coupling, l0_bias, w_ih, w_hh, b_ih, b_hh, rms_w, wk, wo, gamma, beta, konst, kbsel, out):
    with ExitStack() as ctx:
        def sb(name, shape, dt=F32):
            return ctx.enter_context(nc.sbuf_tensor(name, shape, dt))

        def ps(name, shape, dt=F32):
            return ctx.enter_context(nc.psum_tensor(name, shape, dt))

        def sem(name):
            return ctx.enter_context(nc.semaphore(name))

        kon = sb("kon", [P, K_END])
        bselw = sb("bselw", [P, P])
        bselb = sb("bselb", [P, P], BF16)
        coup = sb("coup", [P, R, N])
        cmax = sb("cmax", [P, 3])
        unit = sb("unit", [P, 4])
        w_hi = sb("w_hi", [P, R, R, P], F16)
        w_lo = sb("w_lo", [P, R, R, P], F16)
        condn = sb("condn", [B + 1, N])
        condT = sb("condT", [P, W])
        xfirst = sb("xfirst", [B, FIRST, N])
        xn = sb("xn", [P, TILES, N])
        xT = sb("xT", [P, T, W])
        drv = sb("drv", [P, T, W])
        drv3 = sb("drv3", [P, T, W])
        lb = sb("lb", [P, R])
        dbias = sb("dbias", [P, 2, R])
        q1raw = sb("q1raw", [P, W])
        q1 = sb("q1", [P, W])
        q2 = sb("q2", [P, W])
        q3 = sb("q3", [P, W])
        q4h = sb("q4h", [P, W])
        pu = sb("pu", [P, W])
        pn = sb("pn", [P, 2, W])
        psum_acc = sb("pacc", [P, 3, W])
        t_hi = sb("t_hi", [P, W], F16)
        t_lo = sb("t_lo", [P, W], F16)
        t_full = sb("t_full", [P, W])
        sq = sb("sq", [P, W])
        g3 = sb("g3", [P, W])
        base = sb("base", [P, W])
        gp = sb("gp", [P, 3, W])
        gpf = sb("gpf", [P, W])
        z = sb("z", [P, 3, W])
        zf = sb("zf", [P, W])
        lin3 = sb("lin3", [P, W])
        lin4 = sb("lin4", [P, 2, W])
        linf = sb("linf", [P, 3, W])
        q1f = sb("q1f", [P, W])
        wih = sb("wih", [P, R, 3, N])
        whh = sb("whh", [P, R, 3, N])
        bsrc = sb("bsrc", [P, 4, 64])
        bres = sb("bres", [8, N])
        bprt = sb("bprt", [8, N], BF16)
        bmov = sb("bmov", [P, N], BF16)
        x1 = sb("x1", [P, 2, W])
        hT = sb("hT", [P, W])
        hB = sb("hB", [P, W])
        rz = sb("rz", [P, 2, 64])
        zg = sb("zg", [P, 64])
        zc = sb("zc", [P, 64])
        rn = sb("rn", [P, 64])
        pre = sb("pre", [P, 64])
        ng = sb("ng", [P, 64])
        un = sb("un", [P, 64])
        zh = sb("zh", [P, 64])
        x2 = sb("x2", [P, R, B, T])
        gridn = sb("gridn", [P, 64])
        gridx = sb("gridx", [P, 64])
        ixb = sb("ixb", [P, B * N])
        dist = sb("dist", [P, R, N])
        hat = sb("hat", [P, B * R * N])
        wkn = sb("wkn", [P, 2, N])
        won = sb("won", [P, 2, N])
        wkT = sb("wkT", [P, 2, N])
        woT = sb("woT", [P, 2, N])
        rmsb = sb("rmsb", [P, N])
        qvb = sb("qvb", [P, N])
        qk = sb("qk", [P, N])
        gam = sb("gam", [P, N])
        bet = sb("bet", [P, N])
        x3 = xn
        x3b = drv[:, :, :].rearrange("p t w -> p (t w)").rearrange("p (g n) -> p g n", g=TILES)
        blk = sb("blk", [P, 2, N])
        blkT = sb("blkT", [P, 2, 2, P])
        junk = sb("junk", [P, 2, 2, N])
        ss = sb("ss", [P, 2])
        ms = sb("ms", [P, 2])
        sc = sb("sc", [P, 2])
        rs = sb("rs", [P, 2])
        score = sb("score", [P, 2, 32])
        soft = sb("soft", [P, 2, 4, 32])
        mx = sb("mx", [P, 2, 3, 4])
        attc = sb("attc", [P, 2, 32])
        attw = sb("attw", [P, 2, 4 * P])
        val = sb("val", [P, 2, N])
        st6 = sb("st6", [P, TILES, 6])
        mv = sb("mv", [P, TILES, 2])
        rstd = sb("rstd", [P, TILES])
        vare = sb("vare", [P, TILES])
        nmean = sb("nmean", [P, TILES])
        nbias = sb("nbias", [P, TILES])
        nrm = xT[:, :, :].rearrange("p t w -> p (t w)").rearrange("p (g n) -> p g n", g=TILES)
        yout = drv3[:, :, :].rearrange("p t w -> p (t w)").rearrange("p (g n) -> p g n", g=TILES)

        p_l0 = ps("p_l0", [P, 512])
        p_gru = [ps(f"p_gru{i}", [P, 512]) for i in range(2)]
        p_x = ps("p_x", [P, 512])
        p_x3 = ps("p_x3", [P, 4, 2, N])

        scratch = nc.dram_tensor("grid_scratch", [B, N], F32, kind="Internal").ap()

        ident = kon[:, K_ID:K_ID + P]

        coupT = (p_gru[0], p_x)

        ld_coup, ld_cond, ld_kon = sem("ld_coup"), sem("ld_cond"), sem("ld_kon")
        ld_grid, ld_ih, ld_hh, ld_bias, ld_att, ld_kb = sem("ld_grid"), sem("ld_ih"), sem("ld_hh"), sem("ld_bias"), sem("ld_att"), sem("ld_kb")
        ld_x = [sem(f"ld_x{i}") for i in range(2)]
        ld_first, ld_ix = sem("ld_first"), sem("ld_ix")
        zeroed, grid_step, grid_ready, grid_out = sem("zeroed"), sem("grid_step"), sem("grid_ready"), sem("grid_out")
        cmax_ready, cmax_psum, unit_ready, unit_step = (
            sem("cmax_ready"), sem("cmax_psum"), sem("unit_ready"), sem("unit_step"))
        coupT_psum, w_hi_ready, w_hi_act, w_ready, condT_psum, start_ready = (
            sem("coupT_psum"), sem("w_hi_ready"), sem("w_hi_act"), sem("w_ready"), sem("condT_psum"), sem("start_ready"))
        xT_psum, first_psum, first_ready, xT_ready, dbias_ready, drv_ready = (
            sem("xT_psum"), sem("first_psum"), sem("first_ready"), sem("xT_ready"), sem("dbias_ready"), sem("drv_ready"))
        part_ready, rest_ready, bias_ready, bias_act, qk_ready = sem("part_ready"), sem("rest_ready"), sem("bias_ready"), sem("bias_act"), sem("qk_ready")
        q_ready, q_kept, clipped, t_hi_ready, t_ready, t_lo_ready = (
            sem("q_ready"), sem("q_kept"), sem("clipped"), sem("t_hi_ready"), sem("t_ready"), sem("t_lo_ready"))
        sq_ready, g3_ready, base_ready, coupled = sem("sq_ready"), sem("g3_ready"), sem("base_ready"), sem("coupled")
        lin_done, p_ready = sem("lin_done"), sem("p_ready")
        sp2_ready, sp3_ready, sp4_ready, spf_ready = sem("sp2_ready"), sem("sp3_ready"), sem("sp4_ready"), sem("spf_ready")
        z2_ready, z3_ready, z4_ready, zf_ready, q1f_ready, lfa_ready = (
            sem("z2_ready"), sem("z3_ready"), sem("z4_ready"), sem("zf_ready"), sem("q1f_ready"), sem("lfa_ready"))
        x1_ready, x2_ready, x2_last, zh_ready = sem("x1_ready"), sem("x2_ready"), sem("x2_last"), sem("zh_ready")
        gate_psum, rz_ready, zg_ready, zc_ready, n_ready = sem("gate_psum"), sem("rz_ready"), sem("zg_ready"), sem("zc_ready"), sem("n_ready")
        rn_ready, pre_ready, un_ready, hB_ready, hT_ready = (
            sem("rn_ready"), sem("pre_ready"), sem("un_ready"), sem("hB_ready"), sem("hT_ready"))
        dist_ready, hat_ready, mix_ready = sem("dist_ready"), sem("hat_ready"), sem("mix_ready")
        wT_psum, wT_ready = sem("wT_psum"), sem("wT_ready")
        x3_psum, x3_act, x3_dve, x3b_ready = sem("x3_psum"), sem("x3_act"), sem("x3_dve"), sem("x3b_ready")
        blk_psum, blk_ready, blkT_psum, blkT_ready = sem("blk_psum"), sem("blk_ready"), sem("blkT_psum"), sem("blkT_ready")
        key_psum, val_psum, val_ready, ss_ready, sc_ready, ms_ready, rs_ready, score_ready = (
            sem("key_psum"), sem("val_psum"), sem("val_ready"), sem("ss_ready"), sem("sc_ready"), sem("ms_ready"),
            sem("rs_ready"), sem("score_ready"))
        soft_step, exp_ready, attw_ready, y_psum = sem("soft_step"), sem("exp_ready"), sem("attw_ready"), sem("y_psum")
        stat_done, mv_ready, var_ready, rstd_ready, nbias_ready, nrm_act, nrm_dve, gam_pool, y_pool, y_dve, stored = (
            sem("stat_done"), sem("mv_ready"), sem("var_ready"), sem("rstd_ready"), sem("nbias_ready"), sem("nrm_act"), sem("nrm_dve"),
            sem("gam_pool"), sem("y_pool"), sem("y_dve"), sem("stored"))

        LIN = ["pa", "l3", "pb", "l4a", "lfb", "l4b", "pc", "lfc", "pd"]

        def lin_count(t, name):
            return len(LIN) * t + LIN.index(name) + 1

        q_of = {1: q1, 2: q2, 3: q3, 4: q4h}
        q_psum = p_x[:, 0:W]
        CUBIC = {1: -C / 3, 2: -C / 3, 3: -C / 3, 4: -2 * C / 9}
        SELF = {1: 1.0, 2: 0.0, 3: 0.0, 4: 2 * LFC[4]}

        SOFT = 7

        def add_identity(engine, queue, b):
            queue.wait_ge(hat_ready, (b + 1) * R)
            diag = hat[:, b * R * N:(b + 1) * R * N].rearrange("p (r q n) -> p (r q) n", r=R, n=P)[:, 0:R * R:R + 1, :]
            engine.tensor_tensor(diag, diag, ident.rearrange("p (o n) -> p o n", o=1).broadcast_to([P, R, P]),
                                 ALU.add).then_inc(mix_ready, 1)

        block = ctx.enter_context(nc.Block())

        @block.sync
        def _(sp):
            sp.dma_start(coup[:, :, :], coupling.rearrange("(r p) n -> p r n", r=R)).then_inc(ld_coup, 16)
            sp.dma_start(condn[0:B, :], cond).then_inc(ld_cond, 16)
            sp.dma_start(condn[B:B + 1, :], l0_bias.rearrange("(o n) -> o n", o=1)).then_inc(ld_cond, 16)
            sp.dma_start(xfirst[:, :, :], x[:, 0:FIRST, :]).then_inc(ld_first, 16)
            rows = x.rearrange("(g b) t n -> (b t) g n", b=4)
            for h in range(2):
                sp.dma_start(xn[:, 4 * h:4 * h + 4, :], rows[:, 4 * h:4 * h + 4, :]).then_inc(ld_x[h], 16)
            sp.wait_ge(zeroed, 1)
            bi = b_ih.rearrange("(g r j i) -> j g r i", g=3, r=R, j=J)
            bh = b_hh.rearrange("(g r j i) -> j (g r) i", g=3, r=R, j=J)
            bd = bsrc[:, :, :].rearrange("p g (r i) -> p g r i", r=R)
            sp.dma_start(bd[0:8:2, 0, :, :], bi[:, 2, :, :]).then_inc(ld_bias, 16)
            sp.dma_start(bd[0:8:2, 1:3, :, :], bi[:, 0:2, :, :]).then_inc(ld_bias, 16)
            sp.dma_start(bd[1:8:2, 1:4, :, :].rearrange("p g r i -> p (g r) i"), bh).then_inc(ld_bias, 16)
            sp.dma_start(bselw[:, :], kbsel).then_inc(ld_kb, 16)
            rows = w_ih.rearrange("(r p) m -> p r m", r=R)
            sp.dma_start(wih[:, :, 0, :], rows[:, :, 2 * N:3 * N]).then_inc(ld_ih, 16)
            sp.dma_start(wih[:, :, 1:3, :].rearrange("p r g n -> p r (g n)"), rows[:, :, 0:2 * N]).then_inc(ld_ih, 16)
            sp.dma_start(whh[:, :, :, :].rearrange("p r g n -> p r (g n)"),
                         w_hh.rearrange("(r p) m -> p r m", r=R)).then_inc(ld_hh, 16)
            sp.wait_ge(grid_ready, 1)
            sp.dma_start(scratch.rearrange("b (q f) -> (b q) f", f=64), gridx[:, :]).then_inc(grid_out, 16)
            sp.wait_ge(grid_out, 16)
            flat = scratch.rearrange("b n -> (b n)")
            for h in range(4):
                seg = B * N // 4
                sp.dma_start(ixb[:, seg * h:seg * (h + 1)],
                             flat[seg * h:seg * (h + 1)].partition_broadcast(P)).then_inc(ld_ix, 16)
            sp.dma_start(wkn[:, :, :], wk.rearrange("(c p) h -> p c h", p=P)).then_inc(ld_att, 16)
            sp.dma_start(won[:, :, :], wo.rearrange("(c p) h -> p c h", p=P)).then_inc(ld_att, 16)
            sp.dma_start(rmsb[:, :], rms_w.partition_broadcast(P)).then_inc(ld_att, 16)
            sp.dma_start(gam[:, :], gamma.partition_broadcast(P)).then_inc(ld_att, 16)
            sp.dma_start(bet[:, :], beta.partition_broadcast(P)).then_inc(ld_att, 16)
            sp.dma_start(qvb[:, :], cond[1, :].partition_broadcast(P)).then_inc(ld_att, 16)
            for g in (0, 1, 4, 5):
                if g < 2:
                    sp.wait_ge(y_pool, g + 1)
                else:
                    sp.wait_ge(y_dve, g + 1)
                sp.dma_start(out[4 * g:4 * g + 4, :, :].rearrange("b t n -> (b t) n"), yout[:, g, :]).then_inc(stored, 16)
            sp.wait_ge(stored, 16 * TILES)

        @block.scalar
        def _(act):
            act.dma_start(kon[:, :], konst).then_inc(ld_kon, 16)
            act.dma_start(gridn[:, :], cond.rearrange("b (q f) -> (b q) f", f=64)).then_inc(ld_grid, 16)

            act.wait_ge(condT_psum, 1)
            cp = p_l0[:, 0:R * (B + 1)].rearrange("p (r b) -> p r b", r=R)
            nc.scalar.copy(condT[:, :].rearrange("p (r b) -> p r b", r=R), cp[:, :, 0:B])
            nc.scalar.copy(lb[:, :].rearrange("p (r o) -> p r o", o=1), cp[:, :, B:B + 1]).then_inc(start_ready, 1)

            def x_bank(k):
                h, r = divmod(k, R)
                act.wait_ge(xT_psum, k + 1)
                nc.scalar.copy(xT[:, FIRST:T, 32 * r + 16 * h:32 * r + 16 * h + 16].rearrange("p t b -> p b t"),
                               p_x3[:, k, :, :].rearrange("p g n -> p (g n)").rearrange(
                                   "p (b t) -> p b t", t=T)[:, :, FIRST:T]).then_inc(xT_ready, 1)

            def scale_p(t, which):
                act.wait_ge(p_ready, t + 1)
                if which == "f":
                    nc.scalar.mul(gpf[:, :], pu[:, :], -PU * LFC[0]).then_inc(spf_ready, 1)
                elif which == 2:
                    nc.scalar.mul(gp[:, 0, :], pu[:, :], PU * C).then_inc(sp2_ready, 1)
                else:
                    nc.scalar.mul(gp[:, 1, :], pu[:, :], -PU * L3C[0]).then_inc(sp3_ready, 1)
                    nc.scalar.mul(gp[:, 2, :], pu[:, :], -PU * L4C[0]).then_inc(sp4_ready, 1)

            def hat_dist(b, r):
                nc.scalar.activation(dist[:, r, :], ixb[:, bass.ds(b * N, N)], ACT.Abs,
                                     bias=kon[:, K_FEAT + r:K_FEAT + r + 1]).then_inc(dist_ready, 1)

            def hat_weight(b, r):
                act.wait_ge(dist_ready, b * R + (r + 1))
                nc.scalar.activation(hat[:, bass.ds(b * R * N + r * N, N)], dist[:, r, :], ACT.Relu,
                                     bias=1.0, scale=-1.0).then_inc(hat_ready, 1)

            def bias_part(n):
                if n == 0:
                    act.wait_ge(zeroed, 3)
                    act.wait_ge(ld_bias, 48)
                    nc.scalar.copy(bmov[0:8, :], bsrc[0:8, :, :].rearrange("p g f -> p (g f)")).then_inc(part_ready, 1)
                else:
                    act.wait_ge(rest_ready, 1)
                    nc.scalar.copy(bprt[:, :], bres[:, :]).then_inc(part_ready, 1)
                    nc.scalar.copy(bmov[32:40, :], bres[:, :]).then_inc(bias_act, 1)

            def gate_rz(u):
                act.wait_ge(gate_psum, u + 1)
                nc.scalar.activation(rz[:, :, :].rearrange("p g f -> p (g f)"), p_gru[u_parity[0]][:, 64:192],
                                     ACT.Tanh, scale=0.5).then_inc(rz_ready, 1)
                act.wait_ge(rz_ready, u + 1)
                if u + 2 < T:
                    scale_p(u + 2, "f")
                nc.scalar.activation(zg[:, :], rz[:, 1, :], ACT.Copy, bias=0.5, scale=0.5).then_inc(zg_ready, 1)
                nc.scalar.activation(zc[:, :], rz[:, 1, :], ACT.Copy, bias=-0.5, scale=0.5).then_inc(zc_ready, 1)

            def gate_n(u):
                act.wait_ge(pre_ready, u + 1)
                nc.scalar.activation(ng[:, :], pre[:, :], ACT.Tanh).then_inc(n_ready, 1)

            u_parity = [0]

            def step(t, network, gates, hats):
                u_parity[0] = t % 2
                for s in range(1, 5):
                    if network:
                        src = q1raw[:, :] if s == 1 else q_psum
                        scale = 2.0 if s == 4 else 1.0
                        act.wait_ge(q_ready, t * 4 + s)
                        nc.scalar.activation(t_hi[:, :], src, ACT.Tanh, scale=scale).then_inc(t_hi_ready, 1)
                        nc.scalar.activation(t_full[:, :], src, ACT.Tanh, scale=scale).then_inc(t_ready, 1)
                        if s == 1:
                            act.wait_ge(clipped, t + 1)
                            src = q1[:, :]
                        nc.scalar.activation(sq[:, :], src, ACT.Square, scale=scale).then_inc(sq_ready, 1)
                    if t == 0:
                        x_bank(s - 1)
                    if s == 1:
                        if gates:
                            gate_rz(t - 2)
                        elif network:
                            scale_p(t, "f")
                    if t == 0 and s == 1:
                        bias_part(0)
                    if t == 0 and s == 3:
                        bias_part(1)
                    if s == 4 and t == 0:
                        act.wait_ge(ld_kb, 16)
                        nc.scalar.copy(bselb[:, :], bselw[:, :]).then_inc(bias_act, 1)
                    if s == 2:
                        if gates:
                            gate_n(t - 2)
                        if hats:
                            if t == PEEL:
                                act.wait_ge(ld_ix, 16 * 4)
                            hat_dist(t - PEEL, 0)
                    if s == 3:
                        if hats:
                            hat_weight(t - PEEL, 0)
                            hat_dist(t - PEEL, 1)
                    if s == 4:
                        if hats:
                            hat_weight(t - PEEL, 1)
                        if network and t != T - 1:
                            scale_p(t + 1, 2)
                            scale_p(t + 1, 34)

            act.wait_ge(first_psum, 1)
            nc.scalar.copy(xT[:, 0:FIRST, :].rearrange("p t w -> p (t w)"), p_x3[:, 3, 0, 0:FIRST * W]).then_inc(first_ready, 1)
            scale_p(0, 2)
            scale_p(0, 34)
            act.wait_ge(coupT_psum, 1)
            act.wait_ge(unit_step, 4)
            nc.scalar.activation(w_hi[:, 1, :, :].rearrange("p b n -> p (b n)"), coupT[1][:, 0:N], ACT.Copy,
                                 scale=unit[:, 1:2]).then_inc(w_hi_act, 1)
            for t in range(PEEL):
                step(t, True, t >= 2, False)
            for t in range(PEEL, T):
                step(t, True, True, True)
            def hat_batch(b):
                act.wait_ge(hat_ready, b * R)
                hat_dist(b, 0)
                hat_dist(b, 1)
                hat_weight(b, 0)
                hat_weight(b, 1)

            step(T, False, True, False)
            hat_batch(T - 3)
            act.wait_ge(hat_ready, (T - 2) * R)
            hat_dist(T - 2, 0)
            step(T + 1, False, True, False)
            hat_dist(T - 2, 1)
            hat_weight(T - 2, 0)
            hat_weight(T - 2, 1)
            hat_batch(T - 1)
            act.wait_ge(wT_psum, 1)
            nc.scalar.copy(wkT[:, :, :].rearrange("p c n -> p (c n)"), p_x[:, :]).then_inc(wT_ready, 1)
            act.wait_ge(wT_psum, 2)
            nc.scalar.copy(woT[:, :, :].rearrange("p c n -> p (c n)"), p_l0[:, :]).then_inc(wT_ready, 1)

            def sampled(g):
                act.wait_ge(x3_psum, g + 1)
                nc.scalar.copy(x3[:, g, :], p_x3[:, g % 4, g // 4, :]).then_inc(x3_act, 1)

            def keys(h):
                act.wait_ge(blkT_psum, h + 1)
                nc.scalar.copy(blkT[:, h, :, :].rearrange("p c n -> p (c n)"), p_l0[:, h * N:h * N + N]).then_inc(blkT_ready, 1)

            def squares(h):
                act.wait_ge(key_psum, h + 1)
                nc.scalar.activation(junk[:, h, 0, :], p_gru[h][:, 0:N], ACT.Square, scale=N ** -0.5,
                                     accum_out=ss[:, h:h + 1]).then_inc(ss_ready, 1)
                act.wait_ge(val_psum, h + 1)
                nc.scalar.copy(val[:, h, :], p_gru[1 - h][:, N:2 * N]).then_inc(val_ready, 1)

            def exps(h):
                act.wait_ge(soft_step, SOFT * h + 3)
                nc.scalar.activation(soft[:, h, 2, :], soft[:, h, 1, :], ACT.Exp).then_inc(exp_ready, 1)

            def norms(m):
                act.wait_ge(nbias_ready, m // 2 + 1)
                for g in (2 * m, 2 * m + 1):
                    nc.scalar.activation(nrm[:, g, :], p_x3[:, g % 4, g // 4, :], ACT.Identity, bias=nbias[:, g:g + 1],
                                         scale=rstd[:, g:g + 1]).then_inc(nrm_act, 1)

            def block_sums(h):
                act.wait_ge(blk_psum, h + 1)
                nc.scalar.copy(blk[:, h, :], p_x[:, 0:N]).then_inc(blk_ready, 1)

            sampled(0)
            sampled(2)
            sampled(4)
            block_sums(0)
            keys(0)
            squares(0)
            sampled(6)
            block_sums(1)
            exps(0)
            keys(1)
            squares(1)
            exps(1)
            norms(0)
            norms(2)
            for n, g in enumerate((2, 3, 6, 7)):
                act.wait_ge(y_dve, n + 1)
                act.dma_start(out[4 * g:4 * g + 4, :, :].rearrange("b t n -> (b t) n"), yout[:, g, :]).then_inc(stored, 16)

        @block.tensor
        def _(pe):
            pe.wait_ge(ld_coup, 16)
            pe.wait_ge(ld_kon, 16)
            for rm in range(R):
                for rnn in range(R):
                    ins = nc.tensor.transpose(coupT[rm][:, rnn * P:rnn * P + P], coup[:, rnn, P * rm:P * rm + P], ident)
            ins.then_inc(coupT_psum, 1)
            pe.wait_ge(ld_cond, 32)
            for r in range(R):
                ins = nc.tensor.transpose(p_l0[:, (B + 1) * r:(B + 1) * (r + 1)], condn[:, P * r:P * r + P], kon[0:B + 1, K_ID:K_ID + B + 1])
            ins.then_inc(condT_psum, 1)
            pe.wait_ge(cmax_ready, 1)
            nc.tensor.matmul(p_gru[1][:, 0:P], cmax[:, 0:1].broadcast_to([P, P]), ident, start=True, stop=True).then_inc(cmax_psum, 1)
            pe.wait_ge(ld_first, 16)
            for r in range(R):
                for t in range(FIRST):
                    c0 = (R * t + r) * B
                    ins = nc.tensor.transpose(p_x3[:, 3, 0, c0:c0 + B], xfirst[:, t, P * r:P * r + P], kon[0:B, K_ID:K_ID + B])
            ins.then_inc(first_psum, 1)

            def x_bank(k):
                h, r = divmod(k, R)
                pe.wait_ge(ld_x[h], 16)
                if k == 3:
                    pe.wait_ge(first_ready, 1)
                for g in range(4):
                    ins = nc.tensor.transpose(p_x3[:, k, g // 2, P * (g % 2):P * (g % 2) + P],
                                              xn[:, 4 * h + g, P * r:P * r + P], ident)
                ins.then_inc(xT_psum, 1)

            x_bank(0)

            def couple(w, tt, first, last):
                for rnn in range(R):
                    for rm in range(R):
                        ins = nc.tensor.matmul(p_l0[:, 32 * rnn:32 * rnn + 32], w[:, rm, rnn, :], tt[:, 32 * rm:32 * rm + 32],
                                               start=first and rnn == 0 and rm == 0, stop=last and rm == R - 1,
                                               skip_group_check=True)
                return ins

            def gate_bias(par):
                nc.tensor.matmul(p_gru[par][:, 0:N], bselb[:, :], bmov[:, :], start=True, stop=False, skip_group_check=True)

            def gate_x(par, r):
                for j in range(J):
                    nc.tensor.matmul(p_gru[par][32 * j:32 * j + 32, 0:192], x1[:, par, 32 * r:32 * r + 32],
                                     wih[:, r, :, :].rearrange("p g (q i) -> p g q i", q=R)[:, :, :, 32 * j:32 * j + 32], start=False, stop=False, skip_group_check=True)

            def gate_h(par, r):
                for j in range(J):
                    ins = nc.tensor.matmul(p_gru[par][32 * j:32 * j + 32, 64:256], hT[:, 32 * r:32 * r + 32],
                                           whh[:, r, :, :].rearrange("p g (q i) -> p g q i", q=R)[:, :, :, 32 * j:32 * j + 32], start=False, stop=(r == R - 1),
                                           skip_group_check=True)
                if r == R - 1:
                    ins.then_inc(gate_psum, 1)

            def keep_warm(bank, count):
                for _ in range(count):
                    nc.tensor.matmul(bank, bselb[:, :], bmov[:, :], start=True, stop=True, skip_group_check=True)

            def step(t, network, products):
                par = (t - 1) % 2
                for s in range(1, 5):
                    if network:
                        pe.wait_ge(t_hi_ready, t * 4 + s)
                        if s > 1:
                            pe.wait_ge(q_kept, t * 3 + s - 1)
                        if t == 0 and s == 1:
                            pe.wait_ge(w_hi_ready, 1)
                            pe.wait_ge(w_hi_act, 1)
                        couple(w_hi, t_hi, True, False)
                        if t == 0 and s == 1:
                            pe.wait_ge(w_ready, 1)
                        couple(w_lo, t_hi, False, False)
                    if network:
                        pe.wait_ge(t_lo_ready, t * 4 + s)
                        couple(w_hi, t_lo, False, True).then_inc(coupled, 1)
                        if t == 0 and s < 4:
                            x_bank(s)
                    if s == 1 and products:
                        if t == 1:
                            pe.wait_ge(bias_ready, 1)
                            pe.wait_ge(bias_act, 2)
                        gate_bias(par)
                    if products:
                        if s == 1:
                            if t == 1:
                                pe.wait_ge(ld_ih, 16 * 2)
                            pe.wait_ge(x1_ready, t)
                            gate_x(par, 0)
                        if s == 2:
                            gate_x(par, 1)
                        if s == 3:
                            if t == 1:
                                pe.wait_ge(ld_hh, 16)
                            pe.wait_ge(hT_ready, t)
                            gate_h(par, 0)
                        if s == 4:
                            gate_h(par, 1)

            for t in range(T):
                step(t, True, t >= 1)
            step(T, False, True)

            pe.wait_ge(ld_att, 16 * 6)
            pe.wait_ge(q_ready, 4 * T + 1)
            for n, (src, dst) in enumerate(((wkn, p_x), (won, p_l0))):
                for ch in range(2):
                    for ck in range(2):
                        c0 = ch * N + ck * P
                        ins = nc.tensor.transpose(dst[:, c0:c0 + P], src[:, ck, P * ch:P * ch + P], ident)
                ins.then_inc(wT_psum, 1)

            def sample(g):
                pe.wait_ge(mix_ready, 4 * g + 4)
                if g >= 4:
                    pe.wait_ge(x3_dve if g % 2 else x3_act, (g - 4) // 2 + 1)
                for r in range(R):
                    for j in range(J):
                        b = 4 * g + j
                        ins = nc.tensor.matmul(p_x3[32 * j:32 * j + 32, g % 4, g // 4, :], x2[:, r, b, :],
                                               hat[:, (b * R + r) * N:(b * R + r + 1) * N],
                                               start=(r == 0 and g < 4), stop=(r == R - 1), skip_group_check=True)
                ins.then_inc(x3_psum, 1)

            def block_sums(h):
                pe.wait_ge(wT_ready, 2)
                if h == 1:
                    pe.wait_ge(blk_ready, 1)
                for g in range(4 * h, 4 * h + 4):
                    pe.wait_ge(x3_dve if g % 2 else x3_act, g // 2 + 1)
                    j = g % 4
                    ins = nc.tensor.matmul(p_x[32 * j:32 * j + 32, 0:N], kon[:, K_IND:K_IND + 32],
                                           x3[:, g, :], start=True, stop=True, skip_group_check=True)
                ins.then_inc(blk_psum, 1)

            def turn(h):
                pe.wait_ge(blk_ready, h + 1)
                for c in range(2):
                    c0 = (h * 2 + c) * P
                    ins = nc.tensor.transpose(p_l0[:, c0:c0 + P], blk[:, h, P * c:P * c + P], ident)
                ins.then_inc(blkT_psum, 1)

            def keys(h):
                pe.wait_ge(blkT_ready, h + 1)
                if h == 1:
                    pe.wait_ge(val_ready, 1)
                for c in range(2):
                    ins = nc.tensor.matmul(p_gru[h][:, 0:N], blkT[:, h, c, :], wkT[:, c, :], start=(c == 0), stop=(c == 1),
                                           skip_group_check=True)
                ins.then_inc(key_psum, 1)

            def values(h):
                if h == 1:
                    pe.wait_ge(sc_ready, 1)
                for c in range(2):
                    ins = nc.tensor.matmul(p_gru[1 - h][:, N:2 * N], blkT[:, h, c, :], woT[:, c, :], start=(c == 0), stop=(c == 1),
                                           skip_group_check=True)
                ins.then_inc(val_psum, 1)

            def attend(h):
                pe.wait_ge(val_ready, h + 1)
                for g in range(4):
                    if g % 2 == 0:
                        pe.wait_ge(attw_ready, 2 * h + g // 2 + 1)
                    if h == 1:
                        pe.wait_ge(nrm_act if g < 2 else nrm_dve, g % 2 + 1)
                    nc.tensor.matmul(p_x3[:, g, h, :], attw[:, h, P * g:P * g + P], val[:, h, :], start=False, stop=True,
                                     skip_group_check=True).then_inc(y_psum, 1)

            keep_warm(p_x3[:, 3, 0, :], 5)
            pe.wait_ge(x2_ready, T - 1)
            pe.wait_ge(x2_last, 1)
            for g in range(5):
                sample(g)
            block_sums(0)
            sample(5)
            turn(0)
            sample(6)
            keys(0)
            values(0)
            sample(7)
            block_sums(1)
            turn(1)
            keep_warm(p_x[:, 0:N], 4)
            keys(1)
            attend(0)
            values(1)
            keep_warm(p_l0[:, 0:N], 12)
            attend(1)

        @block.gpsimd
        def _(pool):
            nc.gpsimd.memset(bsrc[:, :, :], 0.0).then_inc(zeroed, 1)
            nc.gpsimd.memset(bmov[:, :], 0.0).then_inc(zeroed, 1)
            nc.gpsimd.memset(score[:, :, :], 0.0).then_inc(zeroed, 1)
            pool.wait_ge(ld_grid, 16)
            nc.gpsimd.tensor_scalar(gridn[:, :], gridn[:, :], 1.0, 0.5 * (N - 1), ALU.add, ALU.mult).then_inc(grid_step, 1)
            pool.wait_ge(grid_step, 1)
            nc.gpsimd.tensor_scalar(gridx[:, :], gridn[:, :], 0.0, float(N - 1), ALU.max, ALU.min).then_inc(grid_ready, 1)
            pool.wait_ge(start_ready, 1)
            nc.gpsimd.tensor_scalar(pu[:, :], condT[:, :], -SHIFT, 1.0 / PU, ALU.add, ALU.mult).then_inc(p_ready, 1)
            for n, c in enumerate((C, C / 3)):
                ins = nc.gpsimd.tensor_scalar(dbias[:, n, :], lb[:, :], -SHIFT, c, ALU.add, ALU.mult)
            ins.then_inc(dbias_ready, 1)
            pool.wait_ge(dbias_ready, 1)
            pool.wait_ge(first_ready, 1)

            driven = [0]

            def drive(first, last, third):
                c, dst = ((C, drv), (C / 3, drv3))[third]
                for r in range(R):
                    ins = nc.gpsimd.tensor_scalar(dst[:, first:last, 32 * r:32 * r + 32], xT[:, first:last, 32 * r:32 * r + 32],
                                                  c, dbias[:, third, r:r + 1], ALU.mult, ALU.add)
                ins.then_inc(drv_ready, 1)
                driven[0] += 1
                pool.wait_ge(drv_ready, driven[0])

            def bias_rest(source, part, out_ap, signal):
                pool.wait_ge(part_ready, part)
                nc.gpsimd.tensor_tensor(out_ap, source, (bmov[0:8, :], bprt[:, :])[part - 1], ALU.subtract).then_inc(signal, 1)

            def z2(t):
                pool.wait_ge(sp2_ready, t + 1)
                nc.gpsimd.tensor_tensor(z[:, 0:1, :], drv[:, bass.ds(t, 1), :], gp[:, 0:1, :], ALU.subtract).then_inc(z2_ready, 1)

            def step(t, network, inputs, gates, hats):
                if network:
                    pool.wait_ge(sp3_ready, t + 1)
                    nc.gpsimd.tensor_tensor(z[:, 1, :], drv[:, t, :], gp[:, 1, :], ALU.subtract).then_inc(z3_ready, 1)
                pool.wait_ge(clipped, t + 1)
                if inputs:
                    if not network:
                        pool.wait_ge(x2_ready, t - 2)
                    nc.gpsimd.tensor_tensor(x1[:, (t - 1) % 2, :], xT[:, t - 1, :], q1[:, :], ALU.add).then_inc(x1_ready, 1)
                if network:
                    pool.wait_ge(sp4_ready, t + 1)
                    nc.gpsimd.tensor_tensor(z[:, 2, :], drv[:, t, :], gp[:, 2, :], ALU.subtract).then_inc(z4_ready, 1)
                    nc.gpsimd.tensor_scalar(q1f[:, :], q1[:, :], LFC[1], 0.0, ALU.mult, ALU.add).then_inc(q1f_ready, 1)
                    if t == 0:
                        drive(0, FIRST, 1)
                    pool.wait_ge(spf_ready, t + 1)
                    nc.gpsimd.tensor_tensor(zf[:, :], drv3[:, t, :], gpf[:, :], ALU.subtract).then_inc(zf_ready, 1)
                    pool.wait_ge(q1f_ready, t + 1)
                    pool.wait_ge(zf_ready, t + 1)
                    nc.gpsimd.tensor_tensor(linf[:, 0, :], zf[:, :], q1f[:, :], ALU.add).then_inc(lfa_ready, 1)
                if t == 0:
                    bias_rest(bsrc[0:8, :, :].rearrange("p g f -> p (g f)"), 1, bres[:, :], rest_ready)
                    pool.wait_ge(rest_ready, 1)
                    bias_rest(bres[:, :], 2, bmov[64:72, :], bias_ready)
                    pool.wait_ge(bias_ready, 1)
                if gates:
                    keep(t)
                if t == 1:
                    pool.wait_ge(xT_ready, 2 * R)
                    drive(FIRST, T, 0)
                elif t in (2, 3):
                    drive((FIRST, HALFWAY)[t - 2], (HALFWAY, T)[t - 2], 1)
                if hats:
                    add_identity(nc.gpsimd, pool, t - PEEL - 1)
                if gates:
                    mix(t)
                if network:
                    pool.wait_ge(lin_done, lin_count(t, "pd"))
                    nc.gpsimd.tensor_scalar(pu[:, :], pn[:, 1, :], (-CLAMP - SHIFT) / PU, (CLAMP - SHIFT) / PU,
                                            ALU.max, ALU.min).then_inc(p_ready, 1)
                    if t != T - 1:
                        z2(t + 1)

            def keep(t):
                pool.wait_ge(zg_ready, t - 1)
                pool.wait_ge(hB_ready, t - 1)
                nc.gpsimd.tensor_tensor(zh[:, :], zg[:, :], hB[:, :], ALU.mult).then_inc(zh_ready, 1)
                if t < T:
                    pool.wait_ge(zc_ready, t - 1)
                    pool.wait_ge(n_ready, t - 1)
                    nc.gpsimd.tensor_tensor(un[:, :], zc[:, :], ng[:, :], ALU.mult).then_inc(un_ready, 1)

            def mix(t):
                pool.wait_ge(hT_ready, t)
                nc.gpsimd.tensor_tensor(x2[:, :, :, bass.ds(t - 2, 1)],
                                        x1[:, t % 2, :].rearrange("p (r b o) -> p r b o", r=R, o=1),
                                        hT[:, :].rearrange("p (r b o) -> p r b o", r=R, o=1), ALU.add).then_inc(x2_ready, 1)

            drive(0, FIRST, 0)
            z2(0)
            for t in range(T + 1):
                step(t, t < T, t >= 1, t >= 2, t > PEEL)
            keep(T + 1)
            pool.wait_ge(ld_att, 16 * 6)
            nc.gpsimd.tensor_tensor(qk[:, :], rmsb[:, :], qvb[:, :], ALU.mult).then_inc(qk_ready, 1)

            def shifted(g):
                pool.wait_ge(x3_dve if g % 2 else x3_act, g // 2 + 1)
                nc.gpsimd.tensor_tensor(x3b[:, g, :], x3[:, g, :], bet[:, :], ALU.add).then_inc(x3b_ready, 1)

            def key_rms(h):
                pool.wait_ge(ms_ready, h + 1)
                nc.gpsimd.tensor_tensor(rs[:, h:h + 1], ms[:, h:h + 1], kon[:, K_HALF:K_HALF + 1], ALU.pow).then_inc(rs_ready, 1)

            def deviation(m):
                two = slice(2 * m, 2 * m + 2)
                pool.wait_ge(var_ready, m + 1)
                nc.gpsimd.tensor_tensor(rstd[:, two], vare[:, two], kon[:, K_HALF:K_HALF + 2], ALU.pow).then_inc(rstd_ready, 1)
                if m % 2 == 0:
                    pool.wait_ge(rstd_ready, m + 1)
                    nc.gpsimd.tensor_tensor(nbias[:, two], nmean[:, two], rstd[:, two], ALU.mult).then_inc(nbias_ready, 1)

            def times_gamma(m):
                for g in (2 * m, 2 * m + 1):
                    pool.wait_ge(nrm_act, m + g % 2 + 1)
                    nc.gpsimd.tensor_tensor(nrm[:, g, :], nrm[:, g, :], gam[:, :], ALU.mult).then_inc(gam_pool, 1)

            def plus_shifted(m):
                for g in (2 * m, 2 * m + 1):
                    pool.wait_ge(gam_pool, g + 1)
                    nc.gpsimd.tensor_tensor(yout[:, g, :], nrm[:, g, :], x3b[:, g, :], ALU.add).then_inc(y_pool, 1)

            for g in range(4):
                shifted(g)
            key_rms(0)
            for g in range(4, 8):
                shifted(g)
            key_rms(1)
            deviation(0)
            times_gamma(0)
            deviation(1)
            plus_shifted(0)
            deviation(2)
            deviation(3)
            times_gamma(2)

        @block.vector
        def _(dve):
            dve.wait_ge(ld_coup, 16)
            nc.vector.tensor_reduce(cmax[:, 0:1], coup[:, :, :].rearrange("p r n -> p (r n)"), AX_X, ALU.max,
                                    apply_absolute_value=True).then_inc(cmax_ready, 1)
            dve.wait_ge(start_ready, 1)
            nc.vector.tensor_copy(q1raw[:, :], condT[:, :]).then_inc(q_ready, 1)
            nc.vector.tensor_copy(q1[:, :], condT[:, :]).then_inc(clipped, 1)
            nc.vector.tensor_copy(hT[:, :], condT[:, :]).then_inc(hT_ready, 1)
            nc.vector.transpose(hB[:, :], condT[:, :]).then_inc(hB_ready, 1)
            dve.wait_ge(cmax_psum, 1)
            nc.vector.tensor_reduce(cmax[:, 1:2], p_gru[1][:, 0:P], AX_X, ALU.max).then_inc(unit_step, 1)
            dve.wait_ge(unit_step, 1)
            nc.vector.tensor_scalar(cmax[:, 2:3], cmax[:, 1:2], 2.0 ** -60, 2.0 ** -14, ALU.max, ALU.mult).then_inc(unit_step, 1)
            dve.wait_ge(unit_step, 2)
            nc.vector.tensor_scalar(unit[:, 0:1].bitcast(I32), cmax[:, 2:3].bitcast(I32), 0x7F800000, None,
                                    ALU.bitwise_and).then_inc(unit_step, 1)
            dve.wait_ge(unit_step, 3)
            nc.vector.reciprocal(unit[:, 1:2], unit[:, 0:1]).then_inc(unit_step, 1)
            nc.vector.tensor_scalar(unit[:, 2:3], unit[:, 0:1], C, None, ALU.mult)
            nc.vector.tensor_scalar(unit[:, 3:4], unit[:, 0:1], C / 3, None, ALU.mult).then_inc(unit_ready, 1)
            dve.wait_ge(coupT_psum, 1)
            dve.wait_ge(unit_step, 4)
            for rm in range(R):
                hi = w_hi[:, rm, :, :].rearrange("p b n -> p (b n)")
                if rm == 0:
                    nc.vector.tensor_scalar(hi, coupT[0][:, 0:N], unit[:, 1:2], None, ALU.mult).then_inc(w_hi_ready, 1)
                    dve.wait_ge(w_hi_ready, 1)
                else:
                    dve.wait_ge(w_hi_act, 1)
                ins = nc.vector.scalar_tensor_tensor(out=w_lo[:, rm, :, :].rearrange("p b n -> p (b n)"), in0=coupT[rm][:, 0:N],
                                                     scalar=unit[:, 1:2], in1=hi, op0=ALU.mult, op1=ALU.subtract)
            ins.then_inc(w_ready, 1)
            dve.wait_ge(unit_ready, 1)

            def linear(out_ap, in0, scalar, in1):
                nc.vector.scalar_tensor_tensor(out=out_ap, in0=in0, scalar=scalar, in1=in1, op0=ALU.mult,
                                               op1=ALU.add).then_inc(lin_done, 1)

            def tanh_low(t, s):
                dve.wait_ge(t_ready, t * 4 + s)
                nc.vector.tensor_tensor(t_lo[:, :], t_full[:, :], t_hi[:, :], ALU.subtract).then_inc(t_lo_ready, 1)

            def cubic(t, s):
                dve.wait_ge(sq_ready, t * 4 + s)
                nc.vector.scalar_tensor_tensor(out=g3[:, :], in0=sq[:, :], scalar=-3.0 + SELF[s] / CUBIC[s], in1=q_of[s][:, :], op0=ALU.add,
                                               op1=ALU.mult).then_inc(g3_ready, 1)

            def base_sum(t, s):
                lin = {1: z[:, 0, :], 2: lin3[:, :], 3: lin4[:, 1, :], 4: linf[:, 2, :]}[s]
                dve.wait_ge(g3_ready, t * 4 + s)
                nc.vector.scalar_tensor_tensor(out=base[:, :], in0=g3[:, :], scalar=CUBIC[s], in1=lin, op0=ALU.mult,
                                               op1=ALU.add).then_inc(base_ready, 1)

            def next_q(t, s):
                dve.wait_ge(base_ready, t * 4 + s)
                dve.wait_ge(coupled, t * 4 + s)
                u = unit[:, 2:3] if s < 4 else unit[:, 3:4]
                dsts = (q1raw[:, :],) if s == 4 else (q_psum, q_of[s + 1][:, :])
                for dst, signal in zip(dsts, (q_ready, q_kept)):
                    nc.vector.scalar_tensor_tensor(out=dst, in0=p_l0[:, 0:W], scalar=u, in1=base[:, :], op0=ALU.mult,
                                                   op1=ALU.add).then_inc(signal, 1)

            def clip(t):
                dve.wait_ge(q_ready, t * 4 + 1)
                nc.vector.tensor_scalar(q1[:, :], q1raw[:, :], -CLAMP, CLAMP, ALU.max, ALU.min).then_inc(clipped, 1)

            def cell_rn(u, par):
                dve.wait_ge(rz_ready, u + 1)
                nc.vector.scalar_tensor_tensor(out=rn[:, :], in0=rz[:, 0, :], scalar=1.0, in1=p_gru[par][:, 192:256],
                                               op0=ALU.add, op1=ALU.mult).then_inc(rn_ready, 1)

            def cell_pre(u, par):
                dve.wait_ge(rn_ready, u + 1)
                nc.vector.scalar_tensor_tensor(out=pre[:, :], in0=rn[:, :], scalar=0.5, in1=p_gru[par][:, 0:64],
                                               op0=ALU.mult, op1=ALU.add).then_inc(pre_ready, 1)

            def cell_un(u):
                dve.wait_ge(n_ready, u + 1)
                nc.vector.scalar_tensor_tensor(out=un[:, :], in0=zg[:, :], scalar=-1.0, in1=ng[:, :], op0=ALU.add,
                                               op1=ALU.mult).then_inc(un_ready, 1)

            def cell_h(u):
                dve.wait_ge(un_ready, u + 1)
                nc.vector.tensor_tensor(hB[:, :], zh[:, :], un[:, :], ALU.subtract).then_inc(hB_ready, 1)

            def cell_t(u):
                dve.wait_ge(hB_ready, u + 2)
                nc.vector.transpose(hT[:, :], hB[:, :]).then_inc(hT_ready, 1)

            def step(t, gates):
                par = t % 2
                if t:
                    clip(t)
                dve.wait_ge(clipped, t + 1)
                dve.wait_ge(p_ready, t + 1)
                linear(psum_acc[:, 0, :], pu[:, :], PU * PNC[0] / PNC[1], q1[:, :])
                tanh_low(t, 1)
                cubic(t, 1)
                dve.wait_ge(z3_ready, t + 1)
                linear(lin3[:, :], q1[:, :], L3C[1], z[:, 1, :])
                base_sum(t, 1)
                if gates:
                    cell_rn(t - 2, par)
                next_q(t, 1)
                if gates:
                    cell_pre(t - 2, par)
                dve.wait_ge(q_kept, t * 3 + 1)
                linear(psum_acc[:, 1, :], psum_acc[:, 0, :], PNC[1] / PNC[2], q2[:, :])
                tanh_low(t, 2)
                cubic(t, 2)
                dve.wait_ge(z4_ready, t + 1)
                linear(lin4[:, 0, :], q1[:, :], L4C[1], z[:, 2, :])
                base_sum(t, 2)
                dve.wait_ge(lfa_ready, t + 1)
                linear(linf[:, 1, :], q2[:, :], LFC[2], linf[:, 0, :])
                next_q(t, 2)
                if gates:
                    cell_h(t - 2)
                dve.wait_ge(q_kept, t * 3 + 2)
                linear(lin4[:, 1, :], q2[:, :], L4C[2], lin4[:, 0, :])
                tanh_low(t, 3)
                cubic(t, 3)
                if gates:
                    cell_t(t - 2)
                base_sum(t, 3)
                linear(psum_acc[:, 2, :], psum_acc[:, 1, :], PNC[2] / PNC[3], q3[:, :])
                next_q(t, 3)
                linear(linf[:, 2, :], q3[:, :], LFC[3], linf[:, 1, :])
                dve.wait_ge(q_kept, t * 3 + 3)
                linear(pn[:, 1, :], psum_acc[:, 2, :], PNC[3] / PU, q4h[:, :])
                tanh_low(t, 4)
                cubic(t, 4)
                base_sum(t, 4)
                next_q(t, 4)

            for t in range(T):
                step(t, t >= 2)
            clip(T)
            for k in (T, T + 1):
                cell_rn(k - 2, k % 2)
                cell_pre(k - 2, k % 2)
                cell_un(k - 2)
                dve.wait_ge(zh_ready, k - 1)
                cell_h(k - 2)
                cell_t(k - 2)
            dve.wait_ge(x1_ready, T)
            dve.wait_ge(hT_ready, T + 1)
            nc.vector.tensor_tensor(x2[:, :, :, T - 1:T], x1[:, (T + 1) % 2, :].rearrange("p (r b o) -> p r b o", r=R, o=1),
                                    hT[:, :].rearrange("p (r b o) -> p r b o", r=R, o=1), ALU.add).then_inc(x2_last, 1)
            for b in range(T - PEEL, T):
                add_identity(nc.vector, dve, b)

            def sampled(g):
                dve.wait_ge(x3_psum, g + 1)
                nc.vector.tensor_copy(x3[:, g, :], p_x3[:, g % 4, g // 4, :]).then_inc(x3_dve, 1)

            def scores(h):
                dve.wait_ge(ss_ready, h + 1)
                nc.vector.tensor_scalar(ms[:, h:h + 1], ss[:, h:h + 1], EPS, None, ALU.add).then_inc(ms_ready, 1)
                dve.wait_ge(qk_ready, 1)
                nc.vector.tensor_tensor_reduce(out=junk[:, h, 1, :], in0=p_gru[h][:, 0:N], in1=qk[:, :], scale=1.0, scalar=0.0,
                                               op0=ALU.mult, op1=ALU.add, accum_out=sc[:, h:h + 1]).then_inc(sc_ready, 1)

            def scores_end(h):
                dve.wait_ge(zeroed, 3)
                dve.wait_ge(sc_ready, h + 1)
                dve.wait_ge(rs_ready, h + 1)
                nc.vector.tensor_tensor(score[:, h, 0:1], sc[:, h:h + 1], rs[:, h:h + 1], ALU.mult).then_inc(score_ready, 1)

            def four(ap):
                return ap.rearrange("p (b n) -> p b n", n=NBLK)

            def spread(ap):
                return ap.rearrange("p (b o) -> p b o", o=1).broadcast_to([P, 4, NBLK])

            def softmax_max(h):
                base_step = SOFT * h
                dve.wait_ge(score_ready, h + 1)
                nc.vector.transpose(soft[:, h, 0, :], score[:, h, :]).then_inc(soft_step, 1)
                dve.wait_ge(soft_step, base_step + 1)
                nc.vector.tensor_reduce(mx[:, h, 0, :], four(soft[:, h, 0, :]), AX_X, ALU.max).then_inc(soft_step, 1)
                dve.wait_ge(soft_step, base_step + 2)
                nc.vector.tensor_tensor(four(soft[:, h, 1, :]), four(soft[:, h, 0, :]), spread(mx[:, h, 0, :]),
                                        ALU.subtract).then_inc(soft_step, 1)

            def softmax_sum(h):
                base_step = SOFT * h
                dve.wait_ge(exp_ready, h + 1)
                nc.vector.tensor_reduce(mx[:, h, 1, :], four(soft[:, h, 2, :]), AX_X, ALU.add).then_inc(soft_step, 1)
                dve.wait_ge(soft_step, base_step + 4)
                nc.vector.reciprocal(mx[:, h, 2, :], mx[:, h, 1, :]).then_inc(soft_step, 1)
                dve.wait_ge(soft_step, base_step + 5)
                nc.vector.tensor_tensor(four(soft[:, h, 3, :]), four(soft[:, h, 2, :]), spread(mx[:, h, 2, :]),
                                        ALU.mult).then_inc(soft_step, 1)
                dve.wait_ge(soft_step, base_step + 6)
                nc.vector.transpose(attc[:, h, :], soft[:, h, 3, :]).then_inc(soft_step, 1)
                dve.wait_ge(soft_step, base_step + 7)
                for two in range(2):
                    member = kon[:, K_BD + 8 * two:K_BD + 8 * two + 8].rearrange("p (b o) -> p b o", o=1).broadcast_to([P, 8, T])
                    nc.vector.tensor_scalar(attw[:, h, 2 * P * two:2 * P * two + 2 * P].rearrange("p (b t) -> p b t", t=T), member,
                                            attc[:, h, 0:1], None, ALU.mult).then_inc(attw_ready, 1)

            def stats(g):
                dve.wait_ge(y_psum, g + 1)
                nc.vector.bn_stats(st6[:, g, :], p_x3[:, g % 4, g // 4, :]).then_inc(stat_done, 1)

            def moments(m):
                dve.wait_ge(stat_done, 2 * m + 2)
                for g in (2 * m, 2 * m + 1):
                    ins = nc.vector.bn_aggr(mv[:, g, :], st6[:, g, :])
                ins.then_inc(mv_ready, 1)

            def shift(m):
                two = slice(2 * m, 2 * m + 2)
                dve.wait_ge(mv_ready, m + 1)
                if m % 2 == 0:
                    nc.vector.tensor_scalar(nmean[:, two], mv[:, two, 0], -1.0, None, ALU.mult)
                nc.vector.tensor_scalar(vare[:, two], mv[:, two, 1], EPS, None, ALU.add).then_inc(var_ready, 1)

            def centre(m):
                for g in (2 * m, 2 * m + 1):
                    nc.vector.scalar_tensor_tensor(out=nrm[:, g, :], in0=p_x3[:, g % 4, g // 4, :], scalar=mv[:, g, 0:1], in1=gam[:, :],
                                                   op0=ALU.subtract, op1=ALU.mult).then_inc(nrm_dve, 1)

            def finish(g):
                dve.wait_ge(rstd_ready, g // 2 + 1)
                dve.wait_ge(x3b_ready, g + 1)
                dve.wait_ge(nrm_dve, g // 4 * 2 + g % 2 + 1)
                nc.vector.scalar_tensor_tensor(out=yout[:, g, :], in0=nrm[:, g, :], scalar=rstd[:, g:g + 1],
                                               in1=x3b[:, g, :], op0=ALU.mult, op1=ALU.add).then_inc(y_dve, 1)

            def plus_shifted(m):
                for g in (2 * m, 2 * m + 1):
                    dve.wait_ge(x3b_ready, g + 1)
                    dve.wait_ge(gam_pool, g - 1)
                    nc.vector.tensor_tensor(yout[:, g, :], nrm[:, g, :], x3b[:, g, :], ALU.add).then_inc(y_dve, 1)

            sampled(1)
            sampled(3)
            sampled(5)
            scores(0)
            scores_end(0)
            sampled(7)
            softmax_max(0)
            softmax_sum(0)
            scores(1)
            stats(0)
            stats(1)
            scores_end(1)
            softmax_max(1)
            moments(0)
            shift(0)
            stats(2)
            softmax_sum(1)
            stats(3)
            moments(1)
            shift(1)
            centre(1)
            stats(4)
            stats(5)
            stats(6)
            moments(2)
            stats(7)
            shift(2)
            finish(2)
            moments(3)
            finish(3)
            shift(3)
            centre(3)
            finish(6)
            finish(7)
            plus_shifted(2)


_INS = ["x", "cond_2048", "L0_cond_coupling", "L0_cond_bias", "L1_cond_W_ih", "L1_cond_W_hh", "L1_cond_b_ih",
        "L1_cond_b_hh", "L3_cond_rms_weight", "L3_cond_Wk", "L3_cond_Wo", "L3_cond_ln_gamma", "L3_cond_ln_beta"]


def kernel(**inputs):
    import concourse.bacc as _bacc
    from concourse.bass_utils import run_bass_kernel_spmd as _run

    nc = _bacc.Bacc("TRN2", target_bir_lowering=False, num_devices=1)
    arrays, args = {}, []
    named = [(n, np.ascontiguousarray(inputs[n])) for n in _INS]
    named += list(zip(("const_tables", "const_bias_rows"), constants()))
    for name, a in named:
        arrays[f"in_{name}_dram"] = a
        args.append(nc.dram_tensor(f"in_{name}_dram", a.shape, mybir.dt.from_np(a.dtype), kind="ExternalInput").ap())
    res = nc.dram_tensor("out_0_dram", (B, T, N), F32, kind="ExternalOutput").ap()
    build(nc, *args, res)
    r = _run(nc, [arrays], core_ids=[0])
    return r.results[0]["out_0_dram"]
```
